# Optimizing a Trainium2 kernel written in Bass

```python
import numpy as np
import jax
import jax.numpy as jnp

def _softmax(x, axis=-1):
    return jax.nn.softmax(x, axis=axis)

def _gelu(x):
    return jax.nn.gelu(x, approximate=True)

def _silu(x):
    return jax.nn.silu(x)

def _sigmoid(x):
    return jax.nn.sigmoid(x)

def _layernorm(x, axis=-1, eps=1e-05):
    m = jnp.mean(x, axis=axis, keepdims=True)
    v = jnp.var(x, axis=axis, keepdims=True)
    return (x - m) / jnp.sqrt(v + eps)

def _scatter_add(tgt, idx, src, axis=0):
    return tgt.at[idx].add(src)

def _segment_sum(src, seg, n):
    return jax.ops.segment_sum(src, seg, n)
kernel_name = 'mk_gnn_preln_d2_gnn_r32_069f83'

def setup_inputs(seed: int=0):
    np.random.seed(seed)
    _w = jnp.asarray

    def _rec_inputs():
        import jax
        import jax.numpy as jnp
        _gk = jax.random.key(seed)
        x = -0.0003713 + 1 * jax.random.normal(jax.random.fold_in(_gk, 1), (3125, 256), jnp.float32)
        src = jax.random.randint(jax.random.fold_in(_gk, 2), (50000,), 0, 3125, jnp.int32)
        dst = jax.random.randint(jax.random.fold_in(_gk, 3), (50000,), 0, 3125, jnp.int32)
        _o = jnp.argsort(dst, stable=True)
        src = src[_o]
        dst = dst[_o]
        edge_type_16 = jax.random.randint(jax.random.fold_in(_gk, 13), (50000,), 0, 16, jnp.int32)
        edge_weight1 = 0.000937891 + 0.999965 * jax.random.normal(jax.random.fold_in(_gk, 14), (50000, 1), jnp.float32)
        return (x, src, dst, edge_type_16, edge_weight1)
    x, src, dst, edge_type_16, edge_weight1 = _rec_inputs()

    def _L0_gnn_setup():
        import jax, jax.numpy as jnp
        import numpy as np
        N_NODES = 50000
        N_EDGES = 25000
        D_IN = 256
        D_OUT = 256
        key = jax.random.key(seed)
        ks = jax.random.split(key, 8)
        feat = jax.random.normal(ks[0], (N_NODES, D_IN), dtype=jnp.float32)
        weight = jax.random.normal(ks[1], (N_EDGES, 1), dtype=jnp.float32)
        src = jax.random.randint(ks[2], (N_EDGES,), 0, N_NODES, dtype=jnp.int32)
        dst = jax.random.randint(ks[3], (N_EDGES,), 0, N_NODES, dtype=jnp.int32)
        W_pool = jax.random.normal(ks[4], (D_IN, D_IN), dtype=jnp.float32) * 0.05
        b_pool = jnp.zeros((D_IN,), dtype=jnp.float32)
        W_self = jax.random.normal(ks[5], (D_OUT, D_IN), dtype=jnp.float32) * 0.05
        b_self = jnp.zeros((D_OUT,), dtype=jnp.float32)
        W_neigh = jax.random.normal(ks[6], (D_OUT, D_IN), dtype=jnp.float32) * 0.05
        b_neigh = jnp.zeros((D_OUT,), dtype=jnp.float32)
        return {'feat': feat, 'weight': weight, 'src': src, 'dst': dst, 'W_pool': W_pool, 'b_pool': b_pool, 'W_self': W_self, 'b_self': b_self, 'W_neigh': W_neigh, 'b_neigh': b_neigh}
    _L0_gnn_all = _L0_gnn_setup()
    _L0_gnn_in = {k: v for k, v in _L0_gnn_all.items() if k in ('W_pool', 'b_pool', 'W_self', 'b_self', 'W_neigh', 'b_neigh')}
    del _L0_gnn_all

    def _L1_gnn_setup():
        import jax, jax.numpy as jnp
        import numpy as np
        N, E, D, ETYPES = (625, 6250, 256, 16)

        def _gelu(x):
            return jax.nn.gelu(x, approximate=False)
        key = jax.random.key(seed)
        ks = jax.random.split(key, 24)
        s = lambda k, shape, fan: (jax.random.normal(k, shape, jnp.float32) / np.sqrt(fan)).astype(jnp.float32)
        inp = {}
        inp['node_embeddings'] = jax.random.normal(ks[0], (N, D), jnp.float32)
        inp['edge_index'] = jax.random.randint(ks[1], (2, E), 0, N, jnp.int64 if jax.config.jax_enable_x64 else jnp.int32)
        inp['edge_type'] = jax.random.randint(ks[2], (E,), 0, ETYPES, jnp.int32)
        inp['task_embedding'] = jax.random.normal(ks[3], (D,), jnp.float32)
        inp['edge_emb'] = s(ks[4], (ETYPES, D), D)
        inp['msg_W'] = s(ks[5], (D, D), D)
        inp['msg_b'] = jnp.zeros((D,), jnp.float32)
        inp['att_W1'] = s(ks[6], (4 * D, D), 4 * D)
        inp['att_b1'] = jnp.zeros((D,), jnp.float32)
        inp['att_W2'] = s(ks[7], (D, 1), D)
        inp['att_b2'] = jnp.zeros((1,), jnp.float32)
        inp['edge_scale'] = jnp.asarray(0.5, jnp.float32)
        inp['ma_W1'] = s(ks[8], (D, 2 * D), D)
        inp['ma_b1'] = jnp.zeros((2 * D,), jnp.float32)
        inp['ma_W2'] = s(ks[9], (2 * D, 2 * D), 2 * D)
        inp['ma_b2'] = jnp.zeros((2 * D,), jnp.float32)
        inp['up_W1'] = s(ks[10], (2 * D, D), 2 * D)
        inp['up_b1'] = jnp.zeros((D,), jnp.float32)
        inp['up_W2'] = s(ks[11], (D, D), D)
        inp['up_b2'] = jnp.zeros((D,), jnp.float32)
        inp['ua_W1'] = s(ks[12], (D, 2 * D), D)
        inp['ua_b1'] = jnp.zeros((2 * D,), jnp.float32)
        inp['ua_W2'] = s(ks[13], (2 * D, 2 * D), 2 * D)
        inp['ua_b2'] = jnp.zeros((2 * D,), jnp.float32)
        inp['ln_g'] = jnp.ones((D,), jnp.float32)
        inp['ln_b'] = jnp.zeros((D,), jnp.float32)
        return inp
    _L1_gnn_all = _L1_gnn_setup()
    _L1_gnn_in = {k: v for k, v in _L1_gnn_all.items() if k in ('task_embedding', 'edge_emb', 'msg_W', 'msg_b', 'att_W1', 'att_b1', 'att_W2', 'att_b2', 'edge_scale', 'ma_W1', 'ma_b1', 'ma_W2', 'ma_b2', 'up_W1', 'up_b1', 'up_W2', 'up_b2', 'ua_W1', 'ua_b1', 'ua_W2', 'ua_b2', 'ln_g', 'ln_b')}
    del _L1_gnn_all
    return {'x': x, 'src': src, 'dst': dst, 'edge_type_16': edge_type_16, 'edge_weight1': edge_weight1, 'L0_gnn_W_pool': _L0_gnn_in['W_pool'], 'L0_gnn_b_pool': _L0_gnn_in['b_pool'], 'L0_gnn_W_self': _L0_gnn_in['W_self'], 'L0_gnn_b_self': _L0_gnn_in['b_self'], 'L0_gnn_W_neigh': _L0_gnn_in['W_neigh'], 'L0_gnn_b_neigh': _L0_gnn_in['b_neigh'], 'L1_gnn_task_embedding': _L1_gnn_in['task_embedding'], 'L1_gnn_edge_emb': _L1_gnn_in['edge_emb'], 'L1_gnn_msg_W': _L1_gnn_in['msg_W'], 'L1_gnn_msg_b': _L1_gnn_in['msg_b'], 'L1_gnn_att_W1': _L1_gnn_in['att_W1'], 'L1_gnn_att_b1': _L1_gnn_in['att_b1'], 'L1_gnn_att_W2': _L1_gnn_in['att_W2'], 'L1_gnn_att_b2': _L1_gnn_in['att_b2'], 'L1_gnn_edge_scale': _L1_gnn_in['edge_scale'], 'L1_gnn_ma_W1': _L1_gnn_in['ma_W1'], 'L1_gnn_ma_b1': _L1_gnn_in['ma_b1'], 'L1_gnn_ma_W2': _L1_gnn_in['ma_W2'], 'L1_gnn_ma_b2': _L1_gnn_in['ma_b2'], 'L1_gnn_up_W1': _L1_gnn_in['up_W1'], 'L1_gnn_up_b1': _L1_gnn_in['up_b1'], 'L1_gnn_up_W2': _L1_gnn_in['up_W2'], 'L1_gnn_up_b2': _L1_gnn_in['up_b2'], 'L1_gnn_ua_W1': _L1_gnn_in['ua_W1'], 'L1_gnn_ua_b1': _L1_gnn_in['ua_b1'], 'L1_gnn_ua_W2': _L1_gnn_in['ua_W2'], 'L1_gnn_ua_b2': _L1_gnn_in['ua_b2'], 'L1_gnn_ln_g': _L1_gnn_in['ln_g'], 'L1_gnn_ln_b': _L1_gnn_in['ln_b']}

def reference(x, src, dst, edge_type_16, edge_weight1, L0_gnn_W_pool, L0_gnn_b_pool, L0_gnn_W_self, L0_gnn_b_self, L0_gnn_W_neigh, L0_gnn_b_neigh, L1_gnn_task_embedding, L1_gnn_edge_emb, L1_gnn_msg_W, L1_gnn_msg_b, L1_gnn_att_W1, L1_gnn_att_b1, L1_gnn_att_W2, L1_gnn_att_b2, L1_gnn_edge_scale, L1_gnn_ma_W1, L1_gnn_ma_b1, L1_gnn_ma_W2, L1_gnn_ma_b2, L1_gnn_up_W1, L1_gnn_up_b1, L1_gnn_up_W2, L1_gnn_up_b2, L1_gnn_ua_W1, L1_gnn_ua_b1, L1_gnn_ua_W2, L1_gnn_ua_b2, L1_gnn_ln_g, L1_gnn_ln_b):
    import jax
    import jax.numpy as jnp

    def _L0_gnn_ref(feat, weight, src, dst, W_pool, b_pool, W_self, b_self, W_neigh, b_neigh):
        import jax, jax.numpy as jnp
        import numpy as np
        N_NODES = 50000
        N_EDGES = 25000
        D_IN = 256
        D_OUT = 256
        n = feat.shape[0]
        h = jax.nn.relu(feat @ W_pool.T + b_pool)
        m = h[src] * weight
        neigh = jax.ops.segment_max(m, dst, num_segments=n)
        deg = jax.ops.segment_sum(jnp.ones((src.shape[0],), feat.dtype), dst, num_segments=n)
        neigh = jnp.where((deg > 0)[:, None], neigh, jnp.zeros((), feat.dtype))
        return feat @ W_self.T + b_self + (neigh @ W_neigh.T + b_neigh)

    def _L1_gnn_ref(node_embeddings, edge_index, edge_type, task_embedding, edge_emb, msg_W, msg_b, att_W1, att_b1, att_W2, att_b2, edge_scale, ma_W1, ma_b1, ma_W2, ma_b2, up_W1, up_b1, up_W2, up_b2, ua_W1, ua_b1, ua_W2, ua_b2, ln_g, ln_b):
        import jax, jax.numpy as jnp
        import numpy as np
        N, E, D, ETYPES = (625, 6250, 256, 16)

        def _gelu(x):
            return jax.nn.gelu(x, approximate=False)
        n_nodes = node_embeddings.shape[0]
        src, dst = (edge_index[0], edge_index[1])
        e = edge_emb[edge_type]
        x_src = node_embeddings[src]
        x_dst = node_embeddings[dst]
        messages = (x_src + e) @ msg_W + msg_b
        task_rep = jnp.broadcast_to(task_embedding, (src.shape[0], task_embedding.shape[0]))
        att_in = jnp.concatenate([x_src, x_dst, e, task_rep], axis=-1)
        edge_delta = jnp.tanh(_gelu(att_in @ att_W1 + att_b1) @ att_W2 + att_b2)
        edge_weight = 1.0 + edge_scale * edge_delta
        ma = _gelu(task_embedding @ ma_W1 + ma_b1) @ ma_W2 + ma_b2
        msg_gamma, msg_beta = (ma[:ma.shape[0] // 2], ma[ma.shape[0] // 2:])
        messages = messages * (1.0 + 0.5 * jnp.tanh(msg_gamma)) + msg_beta
        messages = messages * edge_weight
        agg = jax.ops.segment_sum(messages, dst, num_segments=n_nodes)
        deg = jax.ops.segment_sum(edge_weight[:, 0], dst, num_segments=n_nodes)
        agg = agg / jnp.maximum(deg, 1.0)[:, None]
        ua = _gelu(task_embedding @ ua_W1 + ua_b1) @ ua_W2 + ua_b2
        upd_gamma, upd_beta = (ua[:ua.shape[0] // 2], ua[ua.shape[0] // 2:])
        agg = agg * (1.0 + 0.5 * jnp.tanh(upd_gamma)) + upd_beta
        upd_in = jnp.concatenate([node_embeddings, agg], axis=-1)
        updated = _gelu(upd_in @ up_W1 + up_b1) @ up_W2 + up_b2
        y = node_embeddings + updated
        mu = jnp.mean(y, axis=-1, keepdims=True)
        var = jnp.mean((y - mu) ** 2, axis=-1, keepdims=True)
        return (y - mu) / jnp.sqrt(var + 1e-05) * ln_g + ln_b
    edge_index = jnp.stack([src, dst])
    h = jnp.maximum(_layernorm(x, axis=-1), 0.0)
    x = x + _L0_gnn_ref(h, edge_weight1, src, dst, L0_gnn_W_pool, L0_gnn_b_pool, L0_gnn_W_self, L0_gnn_b_self, L0_gnn_W_neigh, L0_gnn_b_neigh)
    h = jnp.maximum(_layernorm(x, axis=-1), 0.0)
    x = x + _L1_gnn_ref(h, edge_index, edge_type_16, L1_gnn_task_embedding, L1_gnn_edge_emb, L1_gnn_msg_W, L1_gnn_msg_b, L1_gnn_att_W1, L1_gnn_att_b1, L1_gnn_att_W2, L1_gnn_att_b2, L1_gnn_edge_scale, L1_gnn_ma_W1, L1_gnn_ma_b1, L1_gnn_ma_W2, L1_gnn_ma_b2, L1_gnn_up_W1, L1_gnn_up_b1, L1_gnn_up_W2, L1_gnn_up_b2, L1_gnn_ua_W1, L1_gnn_ua_b1, L1_gnn_ua_W2, L1_gnn_ua_b2, L1_gnn_ln_g, L1_gnn_ln_b)
    return x

_drawn_inputs = setup_inputs


def setup_inputs(seed=0):
    import zlib

    import numpy as np

    out = dict(_drawn_inputs(seed))
    spreads = {'L0_gnn_b_pool': (0.0, 0.1),
     'L0_gnn_b_self': (0.0, 0.1),
     'L0_gnn_b_neigh': (0.0, 0.1),
     'L1_gnn_msg_b': (0.0, 0.337),
     'L1_gnn_att_b1': (0.0, 0.8),
     'L1_gnn_ma_b1': (0.0, 0.533),
     'L1_gnn_ma_b2': (0.0, 0.31),
     'L1_gnn_up_b1': (0.0, 0.1),
     'L1_gnn_up_b2': (0.0, 0.1),
     'L1_gnn_ua_b1': (0.0, 0.399),
     'L1_gnn_ua_b2': (0.0, 0.318),
     'L1_gnn_ln_g': (1.0, 0.2),
     'L1_gnn_ln_b': (0.0, 0.1)}
    factors = {'L1_gnn_edge_emb': 8.0, 'L1_gnn_att_W1': 8.0, 'L1_gnn_att_W2': 8.0}
    for name, (base, spread) in spreads.items():
        noise = np.random.default_rng([zlib.crc32(name.encode()), seed]).standard_normal(out[name].shape)
        drawn = base * np.exp(spread * noise) if base else spread * noise
        out[name] = jnp.asarray(drawn.astype(out[name].dtype))
    for name, factor in factors.items():
        out[name] = (out[name] * factor).astype(out[name].dtype)
    return out
```

```python
import concourse.bass as bass
from concourse import mybir
from contextlib import ExitStack
from itertools import count


def gnn_two_layers(nc, A, out):
    fp32, bf16, i32 = mybir.dt.float32, mybir.dt.bfloat16, mybir.dt.int32
    ALU, ACT, AX = mybir.AluOpType, mybir.ActivationFunctionType, mybir.AxisListType

    P = 128
    N, D = A["x"].shape
    E = A["src"].shape[0]
    TY = A["L1_gnn_edge_emb"].shape[0]
    WIN = P - TY
    NT = -(-N // WIN)
    LAST = N - (NT - 1) * WIN
    GN = 4
    NG = NT // GN
    assert NG * GN == NT and D == 2 * P
    ROW = 512
    ER = -(-E // ROW)
    EL = E - (ER - 1) * ROW
    BLK = 32
    FLD = 5
    NB = ER * ROW // BLK
    SG = 4
    RB = P // BLK
    SLOTS = (E + NT * (BLK - 1 + P - 1)) // P
    NGR = -(-SLOTS // SG)
    SLOTS = NGR * SG
    assert NGR % 2 == 1 and NGR % 3 == 2 and NGR <= P
    RC = -(-SLOTS * RB // P)
    NPAD = 4000.0
    NEG = 3.0e38
    GW = SG * P

    blocks_d = nc.dram_tensor("blocks_d", [NB + 1, FLD * BLK], fp32, kind="Internal").ap()
    want_d = nc.dram_tensor("want_d", [RC * P], i32, kind="Internal").ap()
    rec_d = nc.dram_tensor("rec_d", [RC * P, FLD * BLK], fp32, kind="Internal").ap()
    win_d = nc.dram_tensor("win_d", [SLOTS], i32, kind="Internal").ap()
    node_row_d = nc.dram_tensor("node_row_d", [SLOTS * P], bf16, kind="Internal").ap()
    type_row_d = nc.dram_tensor("type_row_d", [SLOTS * P], bf16, kind="Internal").ap()
    start_row_d = nc.dram_tensor("start_row_d", [SLOTS * P], bf16, kind="Internal").ap()
    hp_d = nc.dram_tensor("hp_d", [NT * WIN, D], fp32, kind="Internal").ap()
    ph_d = nc.dram_tensor("ph_d", [NT * WIN, 2 * D], fp32, kind="Internal").ap()

    def bc(ap2, m):
        p, n = ap2.shape
        return ap2.rearrange("p (a n) -> p a n", a=1).to_broadcast([p, m, n])

    def bi(ap2, m):
        p, n = ap2.shape
        return ap2.rearrange("p (n a) -> p n a", a=1).to_broadcast([p, n, m])

    def prow(ap1, p):
        return ap1.rearrange("(a n) -> a n", a=1).to_broadcast([p, ap1.shape[0]])

    top = ExitStack()
    with top:
        def sbt(name, shape, dt, ctx=top):
            return ctx.enter_context(nc.sbuf_tensor(name, shape, dt))

        ps = top.enter_context(nc.psum_tensor("ps", [P, 8 * 512], fp32))
        x = sbt("x_sb", [WIN, NT * D], fp32)
        acc = sbt("acc", [P, (NT + 1) * 2 * P], fp32)
        ident = sbt("ident", [P, P], fp32)
        iof = sbt("iof", [P, P], fp32)
        pcol = sbt("pcol", [P, 1], fp32)
        srcs = sbt("srcs", [P, NGR * SG], i32)
        edgef = sbt("edgef", [P, NGR * 4 * SG], fp32)
        wins = sbt("wins", [1, SLOTS], i32)
        wn = sbt("wn", [P, 2 * D], fp32)
        ACW0 = 2 * WIN
        ACW1 = 2 * WIN + TY
        x3 = x[:, :].rearrange("p (t d) -> p t d", t=NT)
        edgef4 = edgef[:, :].rearrange("p (g f k) -> p g f k", g=NGR, f=4)

        def bank(b, n=1):
            return ps[:, b * 512:(b + n) * 512]

        b1 = ExitStack()
        with b1:
            def s(name, shape, dt):
                return sbt(name, shape, dt, b1)

            def sem(name):
                return b1.enter_context(nc.semaphore(name))

            wraw = s("wraw", [P, 3 * 2 * D], fp32)
            wpT = s("wpT", [P, 2 * D], fp32)
            wsT = s("wsT", [P, 2 * D], fp32)
            bpool = s("bpool", [WIN, D], fp32)
            bself = s("bself", [WIN, D], fp32)
            bneigh = s("bneigh", [WIN, D], fp32)
            nat_i = s("nat_i", [ER, 4 * ROW], i32)
            nat_w = s("nat_w", [ER, ROW], fp32)
            nat_f = s("nat_f", [ER, 2 * ROW], fp32)
            same = s("same", [ER, ROW], fp32)
            blk = s("blk", [ER, ROW * FLD], fp32)
            blk4 = blk[:, :].rearrange("p (b f e) -> p b f e", f=FLD, e=BLK)
            padb = s("padb", [1, FLD * BLK], fp32)
            junk = s("junk", [P, 4 * ROW], fp32)
            cnt = s("cnt", [ER, NT + 1], fp32)
            ones = s("ones", [P, P], fp32)
            io_i = s("io_i", [P, P], i32)
            pc_i = s("pc_i", [P, 1], i32)
            j_i = s("j_i", [NGR, SG], i32)
            r_i = s("r_i", [NGR, SG * RB], i32)
            jf = s("jf", [NGR, SG], fp32)
            rf = s("rf", [NGR, SG * RB], fp32)
            s_f = s("s_f", [NGR, NT + 1], fp32)
            s_i = s("s_i", [NGR, NT + 1], i32)
            fb_i = s("fb_i", [NGR, NT + 1], i32)
            fb = s("fb", [NGR, NT + 1], fp32)
            nsl = s("nsl", [NGR, NT], fp32)
            nsl_i = s("nsl_i", [NGR, NT], i32)
            zero = s("zero", [NGR, NT], fp32)
            cum = s("cum", [NGR, NT], fp32)
            wf = s("wf", [NGR, SG], fp32)
            w_i = s("w_i", [NGR, SG], i32)
            w0 = s("w0", [NGR, SG], fp32)
            cp = s("cp", [NGR, SG], fp32)
            sb0 = s("sb0", [NGR, SG], fp32)
            wantf = s("wantf", [NGR, SG * RB], fp32)
            want_i = s("want_i", [NGR, SG * RB], i32)
            want_pad = s("want_pad", [1, RC * P - SLOTS * RB], i32)
            want = s("want", [P, RC], i32)
            recs = s("recs", [P, RC * FLD * BLK], fp32)
            nat = s("nat", [NGR, SG * RB * FLD * BLK], fp32)
            nat4 = nat[:, :].rearrange("p (b f e) -> p b f e", f=FLD, e=BLK)
            prev = s("prev", [NGR, 1], fp32)
            dsts = s("dsts", [NGR, GW + 1], fp32)
            flds = s("flds", [NGR, FLD * GW], fp32)
            flds3 = flds[:, :].rearrange("p (f e) -> p f e", f=FLD)
            row_n = s("row_n", [NGR, GW], bf16)
            row_t = s("row_t", [NGR, GW], bf16)
            row_s = s("row_s", [NGR, GW], bf16)
            eqp = s("eqp", [NGR, GW], fp32)
            st = s("st", [WIN, GN * 6], fp32)
            mv = s("mv", [WIN, GN * 2], fp32)
            ve = s("ve", [WIN, GN], fp32)
            sd = s("sd", [WIN, GN], fp32)
            rs = s("rs", [WIN, GN], fp32)
            nb = s("nb", [WIN, GN], fp32)
            h = s("h", [WIN, GN * D], fp32)
            hT = s("hT", [P, GN * 2 * WIN], fp32)
            hpb = s("hpb", [WIN, GN * D], fp32)
            hpo = s("hpo", [WIN, GN * D], fp32)
            st3 = st[:, :].rearrange("p (k c) -> p k c", k=GN)
            mv3 = mv[:, :].rearrange("p (k c) -> p k c", k=GN)

            pads_set = sem("pads_set")
            x_pad = sem("x_pad")
            edges_in = sem("edges_in")
            x_in = sem("x_in")
            w_in = sem("w_in")
            bias_in = sem("bias_in")
            io_set = sem("io_set")
            id_set = sem("id_set")
            prep = sem("prep")
            blk_ready = sem("blk_ready")
            blk_out = sem("blk_out")
            cnt_ready = sem("cnt_ready")
            starts_ready = sem("starts_ready")
            starts_read = sem("starts_read")
            want_ready = sem("want_ready")
            want_out = sem("want_out")
            want_in = sem("want_in")
            recs_in = sem("recs_in")
            recs_out = sem("recs_out")
            nat_in = sem("nat_in")
            rows_ready = sem("rows_ready")
            rows_out = sem("rows_out")
            flds_ready = sem("flds_ready")
            cols_ready = sem("cols_ready")
            wT_ps = sem("wT_ps")
            wT_ready = sem("wT_ready")
            bn = sem("bn")
            var_ready = sem("var_ready")
            sd_ready = sem("sd_ready")
            nb_ready = sem("nb_ready")
            rs_ready = sem("rs_ready")
            h_ready = sem("h_ready")
            t_ready = sem("t_ready")
            hT_ready = sem("hT_ready")
            mm_ready = sem("mm_ready")
            bsum_ready = sem("bsum_ready")
            xb_ready = sem("xb_ready")
            evac = sem("evac")
            hpb_free = sem("hpb_free")
            hpo_ready = sem("hpo_ready")
            hpo_out = sem("hpo_out")
            hpo_free = sem("hpo_free")
            hop_v = sem("hop_v")
            hop_a = sem("hop_a")
            hop_p = sem("hop_p")
            block = b1.enter_context(nc.Block())

            @block.sync
            def _(eng):
                eng.wait_ge(pads_set, 1)
                full = (ER - 1) * ROW
                for f, name, off in ((1, "dst", 0), (3, "dst", 1), (0, "src", 0), (2, "edge_type_16", 0)):
                    dst_cols = slice(f * ROW, (f + 1) * ROW)
                    eng.dma_start(nat_i[0:ER - 1, dst_cols],
                                  A[name][off:off + full].rearrange("(p e) -> p e", e=ROW)).then_inc(edges_in, 16)
                    eng.dma_start(nat_i[ER - 1:ER, f * ROW:f * ROW + EL - off],
                                  A[name][off + full:E].rearrange("(p e) -> p e", p=1)).then_inc(edges_in, 16)
                w1 = A["edge_weight1"].rearrange("e o -> (e o)")
                eng.dma_start(nat_w[0:ER - 1, :], w1[0:full].rearrange("(p e) -> p e", e=ROW)).then_inc(edges_in, 16)
                eng.dma_start(nat_w[ER - 1:ER, 0:EL], w1[full:E].rearrange("(p e) -> p e", p=1)).then_inc(edges_in, 16)
                for n, name in enumerate(("L0_gnn_W_pool", "L0_gnn_W_self", "L0_gnn_W_neigh")):
                    eng.dma_start(wraw[:, n * 2 * D:(n + 1) * 2 * D].rearrange("p (o i) -> p o i", o=2),
                                  A[name].rearrange("(o p) i -> p o i", p=P)).then_inc(w_in, 16)
                eng.dma_start(bpool[:, :], prow(A["L0_gnn_b_pool"], WIN)).then_inc(bias_in, 16)
                eng.dma_start(bself[:, :], prow(A["L0_gnn_b_self"], WIN)).then_inc(bias_in, 16)
                eng.dma_start(bneigh[:, :], prow(A["L0_gnn_b_neigh"], WIN)).then_inc(bias_in, 16)
                eng.wait_ge(blk_ready, 2)
                eng.dma_start(blocks_d[0:NB, :].rearrange("(p b) f -> p (b f)", p=ER), blk[:, :]).then_inc(blk_out, 16)
                eng.dma_start(blocks_d[NB:NB + 1, :], padb[:, :]).then_inc(blk_out, 16)
                eng.wait_ge(want_ready, 1)
                eng.dma_start(want_d[0:SLOTS * RB].rearrange("(p c) -> p c", p=NGR), want_i[:, :]).then_inc(want_out, 16)
                eng.dma_start(want_d[SLOTS * RB:RC * P].rearrange("(p c) -> p c", p=1), want_pad[:, :]).then_inc(want_out, 16)
                eng.dma_start(win_d.rearrange("(p c) -> p c", p=NGR), w_i[:, :]).then_inc(want_out, 16)
                eng.wait_ge(want_out, 48)
                with nc.allow_non_contiguous_dma(reason="a small table of indices turned over"):
                    eng.dma_start(want[:, :], want_d.rearrange("(c p) -> p c", p=P)).then_inc(want_in, 16)
                eng.dma_start(wins[:, :], win_d.rearrange("(a c) -> a c", a=1)).then_inc(want_in, 16)
                eng.wait_ge(recs_in, 16 * RC)
                eng.dma_start(rec_d.rearrange("(c p) f -> p c f", p=P),
                              recs[:, :].rearrange("p (c f) -> p c f", c=RC)).then_inc(recs_out, 16)
                eng.wait_ge(recs_out, 16)
                eng.dma_start(nat[:, :], rec_d[0:SLOTS * RB, :].rearrange("(g b) f -> g (b f)", g=NGR)).then_inc(nat_in, 16)
                last_dst = 1 * BLK + BLK - 1
                per = SG * RB * FLD * BLK
                flat = rec_d.rearrange("r f -> (r f)")
                first = (SG * RB - 1) * FLD * BLK + last_dst
                with nc.allow_non_contiguous_dma(reason="one element of each group"):
                    eng.dma_start(prev[1:NGR, :],
                                  flat[0:(NGR - 1) * per].rearrange("(g c) -> g c", c=per)[:, first:first + 1])\
                       .then_inc(nat_in, 16)
                eng.wait_ge(rows_ready, 3)
                for d, t in ((node_row_d, row_n), (type_row_d, row_t), (start_row_d, row_s)):
                    eng.dma_start(d.rearrange("(g e) -> g e", g=NGR), t[:, :]).then_inc(rows_out, 16)
                eng.wait_ge(rows_out, 48)

            @block.scalar
            def _(eng):
                eng.wait_ge(x_pad, 1)
                eng.dma_start(x3[:, 0:NT - 1, :], A["x"][0:(NT - 1) * WIN, :].rearrange("(t p) d -> p t d", p=WIN)).then_inc(x_in, 16)
                eng.dma_start(x3[0:LAST, NT - 1, :], A["x"][(NT - 1) * WIN:N, :]).then_inc(x_in, 16)
                for n, w in enumerate((wpT, wsT, wn)):
                    eng.wait_ge(wT_ps, n + 1)
                    eng.activation(w[:, :], bank(n), ACT.Copy).then_inc(wT_ready, 1)
                eng.sem_inc(hpb_free, 1)

                def h0(i):
                    eng.wait_ge(var_ready, i + 1)
                    eng.activation(sd[:, :], ve[:, :], ACT.Sqrt).then_inc(sd_ready, 1)
                    eng.wait_ge(nb_ready, i + 1)
                    eng.sem_inc(hop_a, 1)
                    for k in range(GN):
                        ins = eng.activation(h[:, k * D:(k + 1) * D], x[:, bass.ds((i * GN + k) * D, D)], ACT.Relu,
                                             scale=rs[:, k:k + 1], bias=nb[:, k:k + 1])
                    ins.then_inc(h_ready, 1)

                def relu(i):
                    eng.wait_ge(evac, 2 * i + 1)
                    eng.wait_ge(hpo_free, i + 1)
                    eng.activation(hpo[:, :], hpb[:, :], ACT.Relu).then_inc(hpo_ready, 1)

                h0(0)
                with eng.Fori(0, NG - 1) as i:
                    h0(i + 1)
                    relu(i)
                    eng.wait_ge(hpo_ready, i + 1)
                    eng.sem_inc(hpb_free, 1)
                relu(NG - 1)

            @block.gpsimd
            def _(eng):
                eng.memset(ident[:, :], 0.0).then_inc(id_set, 1)
                eng.wait_ge(id_set, 1)
                eng.affine_select(out=ident[:, :], in_=ident[:, :], compare_op=ALU.not_equal, fill=1.0,
                                  base=0, pattern=[[-1, P]], channel_multiplier=1).then_inc(id_set, 1)
                eng.iota(io_i[:, :], [[1, P]], base=0, channel_multiplier=0).then_inc(io_set, 1)
                eng.iota(pc_i[:, :], [[0, 1]], base=0, channel_multiplier=1).then_inc(io_set, 1)
                eng.iota(j_i[:, :], [[1, SG]], base=0, channel_multiplier=SG).then_inc(io_set, 1)
                eng.iota(r_i[:, :], [[0, SG], [1, RB]], base=0, channel_multiplier=0).then_inc(io_set, 1)
                eng.wait_ge(bias_in, 48)
                eng.tensor_tensor(bself[:, :], bself[:, :], bneigh[:, :], ALU.add).then_inc(bsum_ready, 1)
                eng.wait_ge(want_in, 32)
                eng.wait_ge(blk_out, 32)
                for c in range(RC):
                    eng.indirect_dma_start(recs[:, c * FLD * BLK:(c + 1) * FLD * BLK], None, blocks_d[:, :],
                                           bass.IndirectOffsetOnAxis(ap=want[:, c:c + 1], axis=0)).then_inc(recs_in, 16)
                eng.wait_ge(bsum_ready, 1)
                eng.sem_inc(hpo_free, 1)
                with eng.Fori(0, NG) as i:
                    eng.wait_ge(h_ready, i + 1)
                    eng.sem_inc(hop_p, 1)
                    g3 = x[:, bass.ds(i * GN * D, GN * D)].rearrange("p (k d) -> p k d", k=GN)
                    eng.tensor_tensor(g3, g3, bc(bself[:, :], GN), ALU.add).then_inc(xb_ready, 1)
                    eng.wait_ge(hpo_ready, i + 1)
                    eng.sem_inc(hop_p, 1)
                    eng.dma_start(hp_d[bass.ds(i * GN * WIN, GN * WIN), :].rearrange("(k p) d -> p k d", p=WIN),
                                  hpo[:, :].rearrange("p (k d) -> p k d", k=GN)).then_inc(hpo_out, 16)
                    eng.wait_ge(hpo_out, 16 * i + 16)
                    eng.sem_inc(hpo_free, 1)

            @block.tensor
            def _(eng):
                eng.wait_ge(id_set, 2)
                eng.wait_ge(w_in, 48)
                for n in range(3):
                    for kin in range(2):
                        for o in range(2):
                            ins = eng.transpose(bank(n)[:, kin * D + o * P:kin * D + o * P + P],
                                                wraw[:, (n * 2 + o) * D + kin * P:(n * 2 + o) * D + kin * P + P], ident[:, :])
                    ins.then_inc(wT_ps, 1)
                eng.wait_ge(cnt_ready, NT)
                eng.matmul(bank(3)[0:NGR, 0:NT + 1], ones[0:ER, 0:NGR], cnt[:, :], start=True, stop=True).then_inc(starts_ready, 1)
                eng.wait_ge(starts_read, 1)
                eng.wait_ge(wT_ready, 3)
                with eng.Fori(0, NG) as i:
                    eng.wait_ge(h_ready, i + 1)
                    for k in range(GN):
                        for hf in range(2):
                            ins = eng.transpose(bank(0, 2)[:, k * 256 + hf * WIN:k * 256 + (hf + 1) * WIN],
                                                h[:, k * D + hf * P:k * D + hf * P + P], ident[0:WIN, 0:WIN])
                    ins.then_inc(t_ready, 1)
                    eng.wait_ge(hT_ready, i + 1)
                    for k in range(GN):
                        for b, w in ((2, wpT), (4, wsT)):
                            for hf in range(2):
                                ins = eng.matmul(bank(b, 2)[0:WIN, k * D:(k + 1) * D],
                                                 hT[:, (k * 2 + hf) * WIN:(k * 2 + hf + 1) * WIN],
                                                 w[:, hf * D:(hf + 1) * D], start=hf == 0, stop=hf == 1)
                    ins.then_inc(mm_ready, 1)
                eng.wait_ge(flds_ready, 1)
                eng.wait_ge(evac, 2 * NG)
                for f in range(FLD):
                    for k in range(SG):
                        ins = eng.transpose(bank(f)[:, k * NGR:(k + 1) * NGR],
                                            flds[:, f * GW + k * P:f * GW + (k + 1) * P], ident[0:NGR, 0:NGR])
                    ins.then_inc(cols_ready, 1)

            @block.vector
            def _(eng):
                eng.memset(nat_i[:, :].rearrange("p (f e) -> p f e", f=4)[:, 0:3:2, :], 0)
                eng.memset(nat_i[:, :].rearrange("p (f e) -> p f e", f=4)[:, 1:4:2, :], int(NPAD))
                eng.memset(nat_w[:, :], 0.0).then_inc(pads_set, 1)
                eng.memset(x[:, (NT - 1) * D:NT * D], 0.0).then_inc(x_pad, 1)
                eng.memset(cnt[:, :], 0.0)
                eng.memset(ones[:, :], 1.0)
                eng.memset(zero[:, :], 0.0)
                eng.memset(padb[:, 0:BLK], 0.0)
                eng.memset(padb[:, BLK:2 * BLK], NPAD)
                eng.memset(padb[:, 2 * BLK:4 * BLK], 0.0)
                eng.memset(padb[:, 4 * BLK:5 * BLK], -NPAD).then_inc(blk_ready, 1)
                eng.memset(want_pad[:, :], NB)
                step = count(1)
                eng.memset(prev[:, :], -1.0).then_inc(prep, 1)
                eng.wait_ge(prep, next(step))
                eng.wait_ge(io_set, 4)
                eng.tensor_copy(iof[:, :], io_i[:, :])
                eng.tensor_copy(pcol[:, :], pc_i[:, :])
                eng.tensor_copy(jf[:, :], j_i[:, :])
                eng.tensor_copy(rf[:, :], r_i[:, :]).then_inc(prep, 1)
                eng.wait_ge(prep, next(step))
                eng.tensor_scalar(zero[:, 0:1], pcol[0:NGR, :], 0.0, None, ALU.mult)
                eng.tensor_scalar(junk[:, 0:1], pcol[:, :], float(WIN), float(-WIN), ALU.is_ge, ALU.mult).then_inc(prep, 1)
                eng.wait_ge(prep, next(step))
                eng.tensor_tensor(pcol[:, :], pcol[:, :], junk[:, 0:1], ALU.add).then_inc(prep, 1)
                eng.wait_ge(prep, next(step))
                eng.wait_ge(edges_in, 160)
                ni = nat_i[:, :].rearrange("p (f e) -> p f e", f=4)
                eng.tensor_copy(nat_f[:, 0:ROW], ni[:, 1, :])
                eng.tensor_copy(nat_f[:, ROW:2 * ROW], ni[:, 3, :]).then_inc(prep, 1)
                eng.wait_ge(prep, next(step))
                def be(ap):
                    return ap.rearrange("p (b e) -> p b e", e=BLK)
                eng.tensor_tensor(same[:, :], nat_f[:, 0:ROW], nat_f[:, ROW:2 * ROW], ALU.is_equal).then_inc(prep, 1)
                eng.tensor_copy(blk4[:, :, 0, :], be(ni[:, 0, :]))
                eng.tensor_copy(blk4[:, :, 1, :], be(nat_f[:, 0:ROW]))
                eng.tensor_copy(blk4[:, :, 2, :], be(ni[:, 2, :]))
                eng.tensor_copy(blk4[:, :, 3, :], be(nat_w[:, :]))
                eng.wait_ge(prep, next(step))
                eng.scalar_tensor_tensor(out=blk4[:, :, 4, :], in0=be(same[:, :]), scalar=-2 * NPAD, in1=be(nat_f[:, 0:ROW]),
                                         op0=ALU.mult, op1=ALU.add).then_inc(blk_ready, 1)
                for w in range(1, NT + 1):
                    if w > 4:
                        eng.wait_ge(cnt_ready, w - 4)
                    eng.tensor_scalar(junk[0:ER, w % 4 * ROW:(w % 4 + 1) * ROW], nat_f[:, 0:ROW], float(w * WIN), 0.0,
                                      ALU.is_lt, ALU.add, accum_out=cnt[:, w:w + 1]).then_inc(cnt_ready, 1)
                eng.wait_ge(starts_ready, 1)
                eng.wait_ge(cnt_ready, NT)
                eng.tensor_copy(s_f[:, :], bank(3)[0:NGR, 0:NT + 1]).then_inc(prep, 1)
                eng.wait_ge(prep, next(step))
                eng.tensor_copy(s_i[:, :], s_f[:, :]).then_inc(starts_read, 1)
                eng.wait_ge(starts_read, 1)
                eng.tensor_scalar(fb_i[:, :], s_i[:, :], BLK.bit_length() - 1, None, ALU.arith_shift_right).then_inc(prep, 1)
                eng.wait_ge(prep, next(step))
                eng.tensor_copy(fb[:, :], fb_i[:, :]).then_inc(prep, 1)
                eng.wait_ge(prep, next(step))
                eng.scalar_tensor_tensor(out=nsl[:, :], in0=fb[:, 0:NT], scalar=float(-BLK), in1=s_f[:, 1:NT + 1],
                                         op0=ALU.mult, op1=ALU.add).then_inc(prep, 1)
                eng.wait_ge(prep, next(step))
                eng.tensor_scalar(nsl_i[:, :], nsl[:, :], float(P - 1), None, ALU.add).then_inc(prep, 1)
                eng.wait_ge(prep, next(step))
                eng.tensor_scalar(nsl_i[:, :], nsl_i[:, :], P.bit_length() - 1, None, ALU.arith_shift_right).then_inc(prep, 1)
                eng.wait_ge(prep, next(step))
                eng.tensor_copy(nsl[:, :], nsl_i[:, :]).then_inc(prep, 1)
                eng.wait_ge(prep, next(step))
                eng.tensor_tensor_scan(cum[:, :], nsl[:, :], zero[:, :], 0.0, ALU.add, ALU.add).then_inc(prep, 1)
                eng.wait_ge(prep, next(step))
                for k in range(SG):
                    eng.tensor_scalar(junk[0:NGR, k * NT:(k + 1) * NT], cum[:, :], jf[:, k:k + 1], 0.0, ALU.is_le, ALU.add,
                                      accum_out=wf[:, k:k + 1])
                    ins = eng.scalar_tensor_tensor(out=junk[0:NGR, 256 + k * NT:256 + (k + 1) * NT], in0=cum[:, :],
                                                   scalar=jf[:, k:k + 1], in1=nsl[:, :], op0=ALU.is_le, op1=ALU.mult,
                                                   accum_out=cp[:, k:k + 1])
                ins.then_inc(prep, 1)
                eng.wait_ge(prep, next(step))
                for k in range(SG):
                    ins = eng.scalar_tensor_tensor(out=junk[0:NGR, 512 + k * (NT + 1):512 + (k + 1) * (NT + 1)], in0=iof[0:NGR, 0:NT + 1],
                                                   scalar=wf[:, k:k + 1], in1=fb[:, :], op0=ALU.is_equal, op1=ALU.mult,
                                                   accum_out=sb0[:, k:k + 1])
                ins.then_inc(prep, 1)
                eng.tensor_scalar(w0[:, :], wf[:, :], float(WIN), None, ALU.mult)
                eng.tensor_copy(w_i[:, :], wf[:, :])
                eng.tensor_tensor(cp[:, :], jf[:, :], cp[:, :], ALU.subtract).then_inc(prep, 1)
                eng.wait_ge(prep, next(step))
                eng.wait_ge(prep, next(step))
                eng.scalar_tensor_tensor(out=sb0[:, :], in0=cp[:, :], scalar=float(RB), in1=sb0[:, :],
                                         op0=ALU.mult, op1=ALU.add).then_inc(prep, 1)
                eng.wait_ge(prep, next(step))
                eng.tensor_tensor(wantf[:, :].rearrange("p (k r) -> p k r", k=SG), bi(sb0[:, :], RB),
                                  rf[:, :].rearrange("p (k r) -> p k r", k=SG), ALU.add).then_inc(prep, 1)
                eng.wait_ge(prep, next(step))
                eng.tensor_scalar(want_i[:, :], wantf[:, :], float(NB), None, ALU.min).then_inc(want_ready, 1)

                def stats(i):
                    for k in range(GN):
                        ins = eng.bn_stats(st3[:, k, :], x[:, bass.ds((i * GN + k) * D, D)])
                    ins.then_inc(bn, 1)
                    eng.wait_ge(bn, 2 * i + 1)
                    eng.sem_inc(hop_v, 1)
                    for k in range(GN):
                        ins = eng.bn_aggr(mv3[:, k, :], st3[:, k, :])
                    ins.then_inc(bn, 1)
                    eng.wait_ge(bn, 2 * i + 2)
                    eng.tensor_scalar(ve[:, :], mv3[:, :, 1], 1e-5, None, ALU.add).then_inc(var_ready, 1)
                    eng.wait_ge(sd_ready, i + 1)
                    eng.reciprocal(rs[:, :], sd[:, :]).then_inc(rs_ready, 1)
                    eng.wait_ge(rs_ready, i + 1)
                    eng.scalar_tensor_tensor(out=nb[:, :], in0=mv3[:, :, 0], scalar=-1.0, in1=rs[:, :],
                                             op0=ALU.mult, op1=ALU.mult).then_inc(nb_ready, 1)

                def turn(i):
                    eng.wait_ge(t_ready, i + 1)
                    src = bank(0, 2).rearrange("p (k c) -> p k c", k=GN)[:, :, 0:2 * WIN]
                    eng.sem_inc(hop_v, 1)
                    eng.tensor_copy(hT[:, :].rearrange("p (k c) -> p k c", k=GN), src).then_inc(hT_ready, 1)

                def take(i):
                    eng.wait_ge(mm_ready, i + 1)
                    eng.wait_ge(hpb_free, i + 1)
                    eng.tensor_tensor(hpb[:, :].rearrange("p (k d) -> p k d", k=GN),
                                      bank(2, 2)[0:WIN, :].rearrange("p (k d) -> p k d", k=GN),
                                      bc(bpool[:, :], GN), ALU.add).then_inc(evac, 1)
                    eng.wait_ge(xb_ready, i + 1)
                    xg = x[:, bass.ds(i * GN * D, GN * D)]
                    eng.tensor_tensor(xg, bank(4, 2)[0:WIN, :], xg, ALU.add).then_inc(evac, 1)

                eng.wait_ge(x_in, 32)
                eng.wait_ge(bias_in, 48)
                stats(0)
                with eng.Fori(0, NG - 1) as i:
                    turn(i)
                    stats(i + 1)
                    take(i)
                turn(NG - 1)
                take(NG - 1)

                eng.wait_ge(nat_in, 32)
                eng.tensor_copy(dsts[:, 0:1], prev[:, :])
                eng.tensor_copy(dsts[:, 1:GW + 1].rearrange("p (b e) -> p b e", e=BLK), nat4[:, :, 1, :])
                for f in (0, 2, 3):
                    ins = eng.tensor_copy(flds3[:, f, :].rearrange("p (b e) -> p b e", e=BLK), nat4[:, :, f, :])
                ins.then_inc(prep, 1)
                w0b = bi(w0[:, :], P)
                eng.wait_ge(prep, next(step))
                eng.tensor_tensor(flds3[:, 1, :].rearrange("p (k e) -> p k e", k=SG),
                                  dsts[:, 1:GW + 1].rearrange("p (k e) -> p k e", k=SG), w0b, ALU.subtract)
                eng.tensor_tensor(eqp[:, :], dsts[:, 1:GW + 1], dsts[:, 0:GW], ALU.is_equal)
                e4 = flds3[:, 4, :]
                eng.tensor_copy(e4.rearrange("p (b e) -> p b e", e=BLK), nat4[:, :, 4, :]).then_inc(prep, 1)
                eng.wait_ge(prep, next(step))
                e4k = e4.rearrange("p (k e) -> p k e", k=SG)
                eng.tensor_tensor(e4k, e4k, w0b, ALU.subtract).then_inc(flds_ready, 1)
                eng.tensor_copy(row_n[:, :], flds3[:, 1, :]).then_inc(rows_ready, 1)
                eng.tensor_copy(row_t[:, :], flds3[:, 2, :]).then_inc(rows_ready, 1)
                eng.tensor_scalar(row_s[:, :], eqp[:, :], -1.0, NEG, ALU.add, ALU.mult).then_inc(rows_ready, 1)
                eng.memset(acc[:, :], 0.0)
                for f in range(FLD):
                    eng.wait_ge(cols_ready, f + 1)
                    src = bank(f)[:, 0:SG * NGR].rearrange("p (k g) -> p g k", k=SG)
                    if f == 0:
                        eng.tensor_copy(srcs[:, :].rearrange("p (g k) -> p g k", k=SG), src)
                    else:
                        at = {3: 0, 4: 1, 2: 2, 1: 3}[f]
                        eng.tensor_copy(edgef4[:, :, at, :], src)

        def has(g):
            return not isinstance(g, int) or 0 <= g < NGR

        def wait(eng, sem, n):
            if not isinstance(n, int) or n > 0:
                eng.wait_ge(sem, n)

        def over_groups(eng, step, ring, lag):
            turns = (NGR - ring) // ring
            for g in range(ring):
                step(g, g, 0)
            with eng.Fori(0, turns) as i:
                for r in range(ring):
                    step(i * ring + (ring + r), r, i + 1)
            for g in range(ring + turns * ring, NGR + lag):
                step(g, g % ring, g // ring)

        b2 = ExitStack()
        with b2:
            def s2(name, shape, dt):
                return [sbt(f"{name}{r}", shape, dt, b2) for r in range(2)]

            def sem2(name):
                return b2.enter_context(nc.semaphore(name))

            gath = s2("gath", [P, SG * D], fp32)
            curi = s2("curi", [P, SG], i32)
            curf = s2("curf", [P, 2 * SG], fp32)
            gw = s2("gw", [P, SG * D], fp32)
            mask = s2("mask", [P, GW], bf16)
            scan = s2("scan", [P, 2 * GW], fp32)
            rowm = s2("rowm", [P, SG * D], fp32)
            ends = s2("ends", [P, SG * WIN], fp32)
            cur_ready = sem2("cur_ready")
            got = [sem2(f"got{r}") for r in range(2)]
            mask_in = [sem2(f"mask_in{r}") for r in range(2)]
            gw_ready = sem2("gw_ready")
            turned = sem2("turned")
            scanned = sem2("scanned")
            unturned = sem2("unturned")
            rows_back = sem2("rows_back")
            ends_ready = sem2("ends_ready")
            selected = sem2("selected")
            summed = sem2("summed")
            hop_p2 = sem2("hop_p2")
            hop_v2 = sem2("hop_v2")
            block = b2.enter_context(nc.Block())

            @block.sync
            def _(eng):
                def step(g, r, n):
                    wait(eng, scanned, (g - 1) * 2)
                    eng.dma_start(mask[r][:, :], prow(start_row_d[bass.ds(g * GW, GW)], P)).then_inc(mask_in[r], 16)
                over_groups(eng, step, 2, 0)

            @block.gpsimd
            def _(eng):
                def step(g, r, n):
                    wait(eng, gw_ready, g - 1)
                    wait(eng, ends_ready, g - 1)
                    eng.sem_inc(hop_p2, 1)
                    eng.tensor_copy(curi[r][:, :], srcs[:, bass.ds(g * SG, SG)])
                    eng.tensor_copy(curf[r][:, :], edgef[:, bass.ds(g * 4 * SG, 2 * SG)]).then_inc(cur_ready, 1)
                    eng.wait_ge(cur_ready, g + 1)
                    eng.sem_inc(hop_p2, 1)
                    for k in range(SG):
                        eng.indirect_dma_start(gath[r][:, k * D:(k + 1) * D], None, hp_d[:, :],
                                               bass.IndirectOffsetOnAxis(ap=curi[r][:, k:k + 1], axis=0)).then_inc(got[r], 16)
                over_groups(eng, step, 2, 0)

            @block.scalar
            def _(eng):
                def step(g, r, n):
                    if has(g):
                        eng.wait_ge(got[r], (n + 1) * (16 * SG))
                        eng.wait_ge(cur_ready, g + 1)
                        wait(eng, turned, g - 1)
                        for k in range(SG):
                            ins = eng.activation(gw[r][:, k * D:(k + 1) * D], gath[r][:, k * D:(k + 1) * D], ACT.Copy,
                                                 scale=curf[r][:, k:k + 1])
                        ins.then_inc(gw_ready, 1)
                    if has(g - 1):
                        wait(eng, selected, g - 2)
                        eng.wait_ge(unturned, g)
                        eng.activation(rowm[1 - r][:, :], bank(4, 2), ACT.Copy).then_inc(rows_back, 1)
                over_groups(eng, step, 2, 1)

            @block.tensor
            def _(eng):
                def step(g, r, n):
                    if has(g):
                        wait(eng, scanned, (g - 1) * 2)
                        eng.wait_ge(gw_ready, g + 1)
                        for k in range(SG):
                            for hf in range(2):
                                ins = eng.transpose(bank(2 * r + hf)[:, k * P:(k + 1) * P],
                                                    gw[r][:, k * D + hf * P:k * D + hf * P + P], ident[:, :])
                        ins.then_inc(turned, 1)
                    if has(g - 1):
                        wait(eng, rows_back, g - 1)
                        eng.wait_ge(scanned, g * 2)
                        for k in range(SG):
                            for hf in range(2):
                                ins = eng.transpose(bank(4, 2)[:, k * D + hf * P:k * D + hf * P + P],
                                                    scan[1 - r][:, hf * GW + k * P:hf * GW + (k + 1) * P], ident[:, :])
                        ins.then_inc(unturned, 1)
                        eng.wait_ge(ends_ready, g)
                        wait(eng, summed, (g - 1) * SG)
                        eng.wait_ge(rows_back, g)
                        for k in range(SG):
                            for hf in range(2):
                                ins = eng.matmul(bank(6, 2)[:, k * 256 + hf * WIN:k * 256 + (hf + 1) * WIN],
                                                 rowm[1 - r][:, k * D + hf * P:k * D + hf * P + P],
                                                 ends[1 - r][:, k * WIN:(k + 1) * WIN], start=True, stop=True)
                        ins.then_inc(selected, 1)
                over_groups(eng, step, 2, 1)

            @block.vector
            def _(eng):
                def step(g, r, n):
                    if has(g - 1):
                        w = [eng.value_load(wins[0:1, bass.ds((g - 1) * SG + k, 1)], min_val=0, max_val=NT) for k in range(SG)]
                    if has(g):
                        eng.wait_ge(mask_in[r], (n + 1) * 16)
                        wait(eng, unturned, g - 1)
                        wait(eng, scanned, g * 2)
                        eng.wait_ge(turned, g + 1)
                        for hf in range(2):
                            start = 0.0 if isinstance(g, int) and g == 0 else scan[1 - r][:, (hf + 1) * GW - 1:(hf + 1) * GW]
                            eng.tensor_tensor_scan(scan[r][:, hf * GW:(hf + 1) * GW], mask[r][:, :], bank(2 * r + hf),
                                                   start, ALU.add, ALU.max).then_inc(scanned, 1)
                        eng.wait_ge(cur_ready, g + 1)
                        for k in range(SG):
                            ins = eng.tensor_scalar(ends[r][:, k * WIN:(k + 1) * WIN], iof[:, 0:WIN],
                                                    curf[r][:, SG + k:SG + k + 1], None, ALU.is_equal)
                        ins.then_inc(ends_ready, 1)
                    if has(g - 1):
                        eng.wait_ge(selected, g)
                        for k in range(SG):
                            to = acc[:, bass.ds(w[k] * ACW0, ACW0)]
                            wait(eng, summed, (g - 1) * SG + k)
                            eng.tensor_tensor(to, bank(6, 2)[:, k * 256:k * 256 + ACW0], to, ALU.add).then_inc(summed, 1)
                over_groups(eng, step, 2, 1)

        def has_tiles(i):
            return not isinstance(i, int) or 0 <= i < NG

        def over_tiles(eng, step, lag=1):
            step(0)
            with eng.Fori(0, NG - 1) as i:
                step(i + 1)
            for i in range(NG, NG + lag):
                step(i)

        qw = sbt("qw", [P, (NT + 1) * 3 * D], bf16)
        qw3 = qw[:, :].rearrange("p (w c) -> p w c", w=NT + 1)
        up = sbt("up", [WIN, NT * D], fp32)
        mc = sbt("mc", [P, 2 * D], fp32)
        em = sbt("em", [TY, D], fp32)
        c2 = sbt("c2", [WIN, D], fp32)
        upw2 = sbt("upw2", [P, 2 * D], fp32)
        w2b = sbt("w2b", [P, D], fp32)
        b2c = sbt("b2c", [P, 1], fp32)
        esc = sbt("esc", [P, 1], fp32)

        b3 = ExitStack()
        with b3:
            def s(name, shape, dt):
                return sbt(name, shape, dt, b3)

            def sem(name):
                return b3.enter_context(nc.semaphore(name))

            attw = s("attw", [P, 8 * D], fp32)
            upw1 = s("upw1", [P, 4 * D], fp32)
            msgw = s("msgw", [P, 2 * D], fp32)
            msgwT = s("msgwT", [P, 2 * D], fp32)
            vw = s("vw", [P, 2 * D], fp32)
            aw1 = s("aw1", [P, 2 * 2 * D], fp32)
            aw2 = s("aw2", [P, 4 * 2 * D], fp32)
            cols = s("cols", [P, 20], fp32)
            emb = s("emb", [TY, D], fp32)
            embT = s("embT", [P, 2 * TY], fp32)
            taskB = s("taskB", [P, 2 * TY], fp32)
            c1B = s("c1B", [P, 2 * TY], fp32)
            ubB = s("ubB", [P, 2 * WIN], fp32)
            ab1 = s("ab1", [TY, D], fp32)
            upb1 = s("upb1", [WIN, D], fp32)
            v1 = s("v1", [P, 4], fp32)
            v2 = s("v2", [P, 8], fp32)
            v3 = s("v3", [P, 4], fp32)
            gain = s("gain", [P, 4], fp32)
            c1 = s("c1", [P, 2], fp32)
            rsb = s("rsb", [TY, D], fp32)
            rres = s("rres", [TY, 2 * D], fp32)
            rpart = s("rpart", [TY, 3 * D], bf16)
            st = s("st_b", [WIN, GN * 6], fp32)
            mv = s("mv_b", [WIN, GN * 2], fp32)
            ve = s("ve_b", [WIN, GN], fp32)
            sd = s("sd_b", [WIN, GN], fp32)
            rs = s("rs_b", [WIN, GN], fp32)
            nb = s("nb_b", [WIN, GN], fp32)
            h = s("h_b", [WIN, GN * D], fp32)
            pb = s("pb", [WIN, GN * D], fp32)
            hT = s("hT_b", [P, GN * 2 * WIN], fp32)
            nT = s("nT", [P, GN * ACW0], fp32)
            qr = s("qr", [WIN, GN * D], fp32)
            st3 = st[:, :].rearrange("p (k c) -> p k c", k=GN)
            mv3 = mv[:, :].rearrange("p (k c) -> p k c", k=GN)
            params_in = sem("params_in")
            ua_free = sem("ua_free")
            ua_in = sem("ua_in")
            tps = sem("tps")
            tv = sem("tv")
            ta = sem("ta")
            r_in = sem("r_in")
            nt_ready = sem("nt_ready")
            n_ready = sem("n_ready")
            x1_ready = sem("x1_ready")
            bn = sem("bn_b")
            var_ready = sem("var_ready_b")
            sd_ready = sem("sd_ready_b")
            rs_ready = sem("rs_ready_b")
            nb_ready = sem("nb_ready_b")
            h_ready = sem("h_ready_b")
            t_ready = sem("t_ready_b")
            hT_ready = sem("hT_ready_b")
            pqu_ready = sem("pqu_ready")
            p_out = sem("p_out")
            q_hi = sem("q_hi")
            u_out = sem("u_out")
            q_res = sem("q_res")
            q_split = sem("q_split")
            h_stored = sem("h_stored")
            p_stored = sem("p_stored")
            hop_s = sem("hop_s_b")
            hop_a = sem("hop_a_b")
            hop_v = sem("hop_v_b")
            hop_p = sem("hop_p_b")
            block = b3.enter_context(nc.Block())
            task, mab1, mab2, uab1, uab2, msgb = (cols[:, a:b] for a, b in ((0, 2), (2, 6), (6, 10), (10, 14), (14, 18), (18, 20)))
            NPAR = 20
            T_TASK, T_EMB, T_MA1, T_MA2, T_UA1, T_UA2, T_GAIN, T_VW, T_RPART, T_MC = range(1, 11)

            @block.sync
            def _(eng):
                def rows(t, name, k):
                    eng.dma_start(t.rearrange("p (k n) -> p k n", k=k),
                                  A[name].rearrange("(k p) n -> p k n", p=P)).then_inc(params_in, 16)
                rows(aw1[:, :], "L1_gnn_ma_W1", 2)
                rows(aw2[:, :], "L1_gnn_ma_W2", 4)
                with nc.allow_non_contiguous_dma(reason="vectors of a few hundred elements as columns"):
                    for t, name in ((task, "L1_gnn_task_embedding"), (mab1, "L1_gnn_ma_b1"), (mab2, "L1_gnn_ma_b2"),
                                    (uab1, "L1_gnn_ua_b1"), (uab2, "L1_gnn_ua_b2"), (msgb, "L1_gnn_msg_b")):
                        eng.dma_start(t, A[name].rearrange("(k p) -> p k", p=P)).then_inc(params_in, 16)
                rows(attw[:, :], "L1_gnn_att_W1", 8)
                rows(upw1[:, :], "L1_gnn_up_W1", 4)
                rows(msgw[:, :], "L1_gnn_msg_W", 2)
                rows(upw2[:, :], "L1_gnn_up_W2", 2)
                eng.dma_start(emb[:, :], A["L1_gnn_edge_emb"]).then_inc(params_in, 16)
                eng.dma_start(ab1[:, :], prow(A["L1_gnn_att_b1"], TY)).then_inc(params_in, 16)
                eng.dma_start(upb1[:, :], prow(A["L1_gnn_up_b1"], WIN)).then_inc(params_in, 16)
                eng.dma_start(w2b[:, :], prow(A["L1_gnn_att_W2"].rearrange("d o -> (d o)"), P)).then_inc(params_in, 16)
                eng.dma_start(b2c[:, :], prow(A["L1_gnn_att_b2"], P)).then_inc(params_in, 16)
                es = A["L1_gnn_edge_scale"]
                eng.dma_start(esc[:, :], prow(es, P)).then_inc(params_in, 16)
                eng.wait_ge(ua_free, 1)
                eng.dma_start(aw1[:, :].rearrange("p (k n) -> p k n", k=2),
                              A["L1_gnn_ua_W1"].rearrange("(k p) n -> p k n", p=P)).then_inc(ua_in, 16)
                eng.dma_start(aw2[:, :].rearrange("p (k n) -> p k n", k=4),
                              A["L1_gnn_ua_W2"].rearrange("(k p) n -> p k n", p=P)).then_inc(ua_in, 16)
                eng.wait_ge(tv, T_RPART)
                eng.dma_start(qw3[WIN:P, :, :], bc(rpart[:, :], NT + 1)).then_inc(r_in, 16)
                eng.wait_ge(r_in, 16)

                def step(i):
                    if has_tiles(i):
                        to = ph_d[bass.ds(i * (GN * WIN), GN * WIN), :].rearrange("(k p) d -> p k d", p=WIN)
                        eng.wait_ge(h_ready, i + 1)
                        eng.sem_inc(hop_s, 1)
                        eng.dma_start(to[:, :, D:2 * D], h[:, :].rearrange("p (k d) -> p k d", k=GN)).then_inc(h_stored, 16)
                        eng.wait_ge(p_out, i + 1)
                        eng.sem_inc(hop_s, 1)
                        eng.dma_start(to[:, :, 0:D], pb[:, :].rearrange("p (k d) -> p k d", k=GN)).then_inc(p_stored, 16)
                over_tiles(eng, step, 0)
                eng.wait_ge(h_stored, 16 * NG)
                eng.wait_ge(p_stored, 16 * NG)

            @block.tensor
            def _(eng):
                eng.wait_ge(params_in, 16 * (NPAR - 2))
                for k in range(2):
                    ins = eng.transpose(bank(0)[:, k * TY:(k + 1) * TY], emb[:, k * P:(k + 1) * P], ident[0:TY, 0:TY])
                for jh in range(2):
                    for ih in range(2):
                        ins = eng.transpose(bank(1)[:, jh * D + ih * P:jh * D + ih * P + P],
                                            msgw[:, ih * D + jh * P:ih * D + jh * P + P], ident[:, :])
                ins.then_inc(tps, 1)

                def affine1(b):
                    for f in range(4):
                        for k in range(2):
                            ins = eng.matmul(bank(b)[:, f:f + 1], aw1[:, k * 2 * D + f * P:k * 2 * D + f * P + P],
                                             task[:, k:k + 1], start=k == 0, stop=k == 1)
                    ins.then_inc(tps, 1)

                def affine2(b):
                    for f in range(4):
                        for k in range(4):
                            ins = eng.matmul(bank(b)[:, f:f + 1], aw2[:, k * 2 * D + f * P:k * 2 * D + f * P + P],
                                             v1[:, k:k + 1], start=k == 0, stop=k == 3)
                    ins.then_inc(tps, 1)
                affine1(2)
                eng.wait_ge(tv, T_EMB)
                for k in range(2):
                    eng.matmul(bank(3)[0:TY, 0:D], embT[:, k * TY:(k + 1) * TY], attw[:, (4 + k) * D:(5 + k) * D], start=k == 0, stop=False)
                for k in range(2):
                    ins = eng.matmul(bank(3)[0:TY, 0:D], taskB[:, k * TY:(k + 1) * TY], attw[:, (6 + k) * D:(7 + k) * D],
                                     start=False, stop=k == 1)
                ins.then_inc(tps, 1)
                eng.wait_ge(ta, 1)
                affine2(4)
                eng.wait_ge(ua_in, 32)
                affine1(5)
                eng.wait_ge(ta, 2)
                affine2(6)
                eng.wait_ge(tv, T_VW)
                for ih in range(2):
                    for jh in range(2):
                        ins = eng.matmul(bank(7)[:, ih * D:(ih + 1) * D], msgwT[:, jh * D + ih * P:jh * D + ih * P + P],
                                         vw[:, jh * D:(jh + 1) * D], start=jh == 0, stop=jh == 1)
                ins.then_inc(tps, 1)
                for jh in range(2):
                    ins = eng.matmul(bank(1)[0:WIN, 0:D], ubB[:, jh * WIN:(jh + 1) * WIN], upw1[:, (2 + jh) * D:(3 + jh) * D],
                                     start=jh == 0, stop=jh == 1)
                ins.then_inc(tps, 1)
                eng.wait_ge(tv, T_MC)
                for k in range(2):
                    eng.matmul(bank(2)[0:TY, 0:D], embT[:, k * TY:(k + 1) * TY], mc[:, k * D:(k + 1) * D], start=k == 0, stop=False)
                for jh in range(2):
                    ins = eng.matmul(bank(2)[0:TY, 0:D], c1B[:, jh * TY:(jh + 1) * TY], upw1[:, (2 + jh) * D:(3 + jh) * D],
                                     start=False, stop=jh == 1)
                ins.then_inc(tps, 1)
                eng.wait_ge(tv, T_MC + 1)

                def step(i):
                    if has_tiles(i - 1):
                        eng.wait_ge(h_ready, i)
                        for k in range(GN):
                            for hf in range(2):
                                ins = eng.transpose(bank(0, 2)[:, k * 256 + hf * WIN:k * 256 + (hf + 1) * WIN],
                                                    h[:, k * D + hf * P:k * D + hf * P + P], ident[0:WIN, 0:WIN])
                        ins.then_inc(t_ready, 1)
                        eng.wait_ge(hT_ready, i)
                    if has_tiles(i):
                        eng.wait_ge(nt_ready, i + 1)
                        for k in range(GN):
                            for hf in range(2):
                                ins = eng.matmul(bank(0, 2)[0:WIN, k * D:(k + 1) * D],
                                                 nT[:, k * ACW0 + hf * WIN:k * ACW0 + (hf + 1) * WIN],
                                                 wn[:, hf * D:(hf + 1) * D], start=hf == 0, stop=hf == 1)
                        ins.then_inc(n_ready, 1)
                    if has_tiles(i - 1):
                        wait(eng, u_out, i - 1)
                        wait(eng, q_res, i - 1)
                        for b, w in ((4, attw[:, 2 * D:4 * D]), (2, attw[:, 0:2 * D]), (6, upw1[:, 0:2 * D])):
                            for k in range(GN):
                                for hf in range(2):
                                    ins = eng.matmul(bank(b, 2)[0:WIN, k * D:(k + 1) * D],
                                                     hT[:, (k * 2 + hf) * WIN:(k * 2 + hf + 1) * WIN],
                                                     w[:, hf * D:(hf + 1) * D], start=hf == 0, stop=hf == 1)
                            ins.then_inc(pqu_ready, 1)
                over_tiles(eng, step)

            @block.scalar
            def _(eng):
                for n in range(2):
                    eng.wait_ge(tv, (T_MA1, T_UA1)[n])
                    eng.activation(v1[:, :], v3[:, :], ACT.Gelu).then_inc(ta, 1)
                eng.wait_ge(tv, T_UA2)
                eng.activation(gain[:, 0:2], v2[:, 0:2], ACT.Tanh)
                eng.activation(gain[:, 2:4], v2[:, 4:6], ACT.Tanh).then_inc(ta, 1)

                def step(i):
                    if has_tiles(i):
                        eng.wait_ge(var_ready, i + 1)
                        eng.activation(sd[:, :], ve[:, :], ACT.Sqrt).then_inc(sd_ready, 1)
                        wait(eng, h_stored, i * 16)
                        eng.wait_ge(nb_ready, i + 1)
                        eng.sem_inc(hop_a, 1)
                        for k in range(GN):
                            ins = eng.activation(h[:, k * D:(k + 1) * D], x[:, bass.ds((i * GN + k) * D, D)], ACT.Relu,
                                                 scale=rs[:, k:k + 1], bias=nb[:, k:k + 1])
                        ins.then_inc(h_ready, 1)
                    if has_tiles(i - 1):
                        eng.wait_ge(pqu_ready, i * 3 - 2)
                        eng.sem_inc(hop_a, 1)
                        eng.activation(qw3[0:WIN, bass.ds((i - 1) * GN, GN), 0:D],
                                       bank(4, 2)[0:WIN, :].rearrange("p (k d) -> p k d", k=GN), ACT.Copy).then_inc(q_hi, 1)
                        eng.wait_ge(pqu_ready, i * 3 - 1)
                        wait(eng, p_stored, (i - 1) * 16)
                        eng.activation(pb[:, :], bank(2, 2)[0:WIN, :], ACT.Copy).then_inc(p_out, 1)
                        eng.wait_ge(pqu_ready, i * 3)
                        eng.sem_inc(hop_a, 1)
                        eng.activation(up[:, bass.ds((i - 1) * (GN * D), GN * D)], bank(6, 2)[0:WIN, :], ACT.Copy).then_inc(u_out, 1)
                over_tiles(eng, step)

            @block.gpsimd
            def _(eng):
                def step(i):
                    if has_tiles(i):
                        wait(eng, n_ready, i)
                        eng.sem_inc(hop_p, 1)
                        eng.tensor_copy(nT[:, :], acc[:, bass.ds(i * (GN * ACW0), GN * ACW0)]).then_inc(nt_ready, 1)
                    if has_tiles(i - 1):
                        i = i - 1
                        win = bass.ds(i * GN, GN)
                        qr3 = qr[:, :].rearrange("p (k d) -> p k d", k=GN)
                        eng.wait_ge(q_res, i + 1)
                        eng.sem_inc(hop_p, 1)
                        eng.tensor_copy(qw3[0:WIN, win, D:2 * D], qr3).then_inc(q_split, 1)
                        eng.wait_ge(q_split, i * 3 + 1)
                        eng.sem_inc(hop_p, 1)
                        eng.tensor_tensor(qr3, qr3, qw3[0:WIN, win, D:2 * D], ALU.subtract).then_inc(q_split, 1)
                        eng.wait_ge(q_split, i * 3 + 2)
                        eng.sem_inc(hop_p, 1)
                        eng.tensor_copy(qw3[0:WIN, win, 2 * D:3 * D], qr3).then_inc(q_split, 1)
                over_tiles(eng, step)

            @block.vector
            def _(eng):
                one = count(1)
                done = sem("done_b")
                eng.memset(qw[:, NT * 3 * D:(NT + 1) * 3 * D], 0.0)
                eng.wait_ge(params_in, 16 * (NPAR - 2))
                for k in range(2):
                    ins = eng.tensor_copy(taskB[:, k * TY:(k + 1) * TY], task[:, k:k + 1].to_broadcast([P, TY]))
                ins.then_inc(tv, 1)
                eng.wait_ge(tps, 1)
                eng.tensor_copy(msgwT[:, :], bank(1))
                eng.tensor_copy(embT[:, :], bank(0)[:, 0:2 * TY]).then_inc(tv, 1)
                eng.wait_ge(tps, 2)
                eng.tensor_tensor(v3[:, :], bank(2)[:, 0:4], mab1, ALU.add).then_inc(tv, 1)
                eng.wait_ge(tps, 4)
                eng.tensor_tensor(v2[:, 0:4], bank(4)[:, 0:4], mab2, ALU.add).then_inc(tv, 1)
                eng.wait_ge(tv, T_MA2)
                eng.sem_inc(ua_free, 1)
                eng.wait_ge(tps, 5)
                eng.wait_ge(ta, 1)
                eng.tensor_tensor(v3[:, :], bank(5)[:, 0:4], uab1, ALU.add).then_inc(tv, 1)
                eng.wait_ge(tps, 6)
                eng.tensor_tensor(v2[:, 4:8], bank(6)[:, 0:4], uab2, ALU.add).then_inc(tv, 1)
                eng.wait_ge(ta, 3)
                eng.tensor_scalar(gain[:, :], gain[:, :], 0.5, 1.0, ALU.mult, ALU.add).then_inc(tv, 1)
                eng.wait_ge(tv, T_GAIN)
                eng.tensor_tensor(v3[:, 0:2], gain[:, 0:2], gain[:, 2:4], ALU.mult)
                eng.tensor_tensor(c1[:, :], msgb, gain[:, 0:2], ALU.mult)
                for k in range(2):
                    ins = eng.tensor_copy(ubB[:, k * WIN:(k + 1) * WIN], v2[:, 6 + k:7 + k].to_broadcast([P, WIN]))
                ins.then_inc(done, 1)
                eng.wait_ge(done, next(one))
                for k in range(2):
                    eng.tensor_scalar(vw[:, k * D:(k + 1) * D], upw1[:, (2 + k) * D:(3 + k) * D], v3[:, k:k + 1], None, ALU.mult)
                eng.tensor_tensor(c1[:, :], c1[:, :], v2[:, 2:4], ALU.add).then_inc(done, 1)
                eng.wait_ge(done, next(one))
                eng.tensor_tensor(c1[:, :], c1[:, :], gain[:, 2:4], ALU.mult).then_inc(done, 1)
                eng.wait_ge(done, next(one))
                for k in range(2):
                    ins = eng.tensor_copy(c1B[:, k * TY:(k + 1) * TY], c1[:, k:k + 1].to_broadcast([P, TY]))
                ins.then_inc(tv, 1)
                eng.wait_ge(tps, 3)
                eng.tensor_tensor(rsb[:, :], bank(3)[0:TY, 0:D], ab1[:, :], ALU.add).then_inc(done, 1)
                eng.wait_ge(done, next(one))
                eng.tensor_copy(rpart[:, 0:D], rsb[:, :]).then_inc(done, 1)
                eng.wait_ge(done, next(one))
                eng.tensor_tensor(rres[:, 0:D], rsb[:, :], rpart[:, 0:D], ALU.subtract).then_inc(done, 1)
                eng.wait_ge(done, next(one))
                eng.tensor_copy(rpart[:, D:2 * D], rres[:, 0:D]).then_inc(done, 1)
                eng.wait_ge(done, next(one))
                eng.tensor_tensor(rres[:, D:2 * D], rres[:, 0:D], rpart[:, D:2 * D], ALU.subtract).then_inc(done, 1)
                eng.wait_ge(done, next(one))
                eng.tensor_copy(rpart[:, 2 * D:3 * D], rres[:, D:2 * D]).then_inc(tv, 1)
                eng.wait_ge(tps, 8)
                eng.tensor_tensor(c2[:, :], bank(1)[0:WIN, 0:D], upb1[:, :], ALU.add)
                eng.tensor_copy(mc[:, :], bank(7)).then_inc(tv, 1)
                eng.wait_ge(tps, 9)
                eng.tensor_copy(em[:, :], bank(2)[0:TY, 0:D]).then_inc(tv, 1)

                def step(i):
                    if has_tiles(i - 1):
                        eng.wait_ge(t_ready, i)
                        eng.sem_inc(hop_v, 1)
                        eng.tensor_copy(hT[:, :].rearrange("p (k c) -> p k c", k=GN),
                                        bank(0, 2).rearrange("p (k c) -> p k c", k=GN)[:, :, 0:2 * WIN]).then_inc(hT_ready, 1)
                    if has_tiles(i):
                        eng.wait_ge(n_ready, i + 1)
                        xg = x[:, bass.ds(i * (GN * D), GN * D)]
                        eng.tensor_tensor(xg, bank(0, 2)[0:WIN, :], xg, ALU.add).then_inc(x1_ready, 1)
                        eng.wait_ge(x1_ready, i + 1)
                        eng.sem_inc(hop_v, 1)
                        for k in range(GN):
                            ins = eng.bn_stats(st3[:, k, :], x[:, bass.ds((i * GN + k) * D, D)])
                        ins.then_inc(bn, 1)
                        eng.wait_ge(bn, 2 * i + 1)
                        eng.sem_inc(hop_v, 1)
                        for k in range(GN):
                            ins = eng.bn_aggr(mv3[:, k, :], st3[:, k, :])
                        ins.then_inc(bn, 1)
                        eng.wait_ge(bn, 2 * i + 2)
                        eng.tensor_scalar(ve[:, :], mv3[:, :, 1], 1e-5, None, ALU.add).then_inc(var_ready, 1)
                        eng.wait_ge(sd_ready, i + 1)
                        eng.reciprocal(rs[:, :], sd[:, :]).then_inc(rs_ready, 1)
                        eng.wait_ge(rs_ready, i + 1)
                        eng.scalar_tensor_tensor(out=nb[:, :], in0=mv3[:, :, 0], scalar=-1.0, in1=rs[:, :],
                                                 op0=ALU.mult, op1=ALU.mult).then_inc(nb_ready, 1)
                    if has_tiles(i - 1):
                        wait(eng, q_split, (i - 1) * 3)
                        eng.wait_ge(q_hi, i)
                        eng.tensor_tensor(qr[:, :].rearrange("p (k d) -> p k d", k=GN),
                                          bank(4, 2)[0:WIN, :].rearrange("p (k d) -> p k d", k=GN),
                                          qw3[0:WIN, bass.ds((i - 1) * GN, GN), 0:D], ALU.subtract).then_inc(q_res, 1)
                over_tiles(eng, step)

        b4 = ExitStack()
        with b4:
            RING = 3

            def s3(name, shape, dt):
                return [sbt(f"{name}{r}", shape, dt, b4) for r in range(RING)]

            def sem4(name):
                return b4.enter_context(nc.semaphore(name))

            gath = s3("gath1_", [P, SG * 2 * D], fp32)
            key = s3("key", [P, GW], bf16)
            hot = s3("hot", [P, GW], bf16)
            z = s3("z", [P, SG * D], fp32)
            place = s3("place", [P, SG * P], fp32)
            types = s3("types", [P, SG * TY], fp32)
            curi = s3("curi1_", [P, SG], i32)
            curf = s3("curf1_", [P, 2 * SG], fp32)
            logit = s3("logit", [P, SG], fp32)
            delta = s3("delta", [P, SG], fp32)
            ew = s3("ew", [P, SG], fp32)
            zeroed = sem4("zeroed")
            cur_ready = sem4("cur_ready1")
            got = [sem4(f"got1_{r}") for r in range(RING)]
            key_in = [sem4(f"key_in{r}") for r in range(RING)]
            hot_ready = sem4("hot_ready")
            qr_ready = sem4("qr_ready")
            z_ready = sem4("z_ready")
            gelu_ready = sem4("gelu_ready")
            logit_ready = sem4("logit_ready")
            delta_ready = sem4("delta_ready")
            ew_ready = sem4("ew_ready")
            place_ready = sem4("place_ready")
            sums_ready = sem4("sums_ready")
            summed = sem4("summed1")
            hop_p = sem4("hop_p4")
            block = b4.enter_context(nc.Block())

            @block.sync
            def _(eng):
                def step(g, r, n):
                    wait(eng, hot_ready, g - 2)
                    eng.dma_start(key[r][0:WIN, :], prow(node_row_d[bass.ds(g * GW, GW)], WIN)).then_inc(key_in[r], 16)
                    eng.dma_start(key[r][WIN:P, :], prow(type_row_d[bass.ds(g * GW, GW)], TY)).then_inc(key_in[r], 16)
                over_groups(eng, step, RING, 0)

            @block.gpsimd
            def _(eng):
                def step(g, r, n):
                    wait(eng, sums_ready, g - 2)
                    eng.sem_inc(hop_p, 1)
                    eng.tensor_copy(curi[r][:, :], srcs[:, bass.ds(g * SG, SG)])
                    eng.tensor_copy(curf[r][:, :], edgef[:, bass.ds(g * (4 * SG) + 2 * SG, 2 * SG)]).then_inc(cur_ready, 1)
                    eng.wait_ge(cur_ready, g + 1)
                    eng.sem_inc(hop_p, 1)
                    for k in range(SG):
                        eng.indirect_dma_start(gath[r][:, k * 2 * D:(k + 1) * 2 * D], None, ph_d[:, :],
                                               bass.IndirectOffsetOnAxis(ap=curi[r][:, k:k + 1], axis=0)).then_inc(got[r], 16)
                over_groups(eng, step, RING, 0)

            @block.scalar
            def _(eng):
                def step(g, r, n):
                    if has(g - 1):
                        q = (r - 1) % RING
                        eng.wait_ge(logit_ready, g)
                        eng.activation(delta[q][:, :], logit[q][:, :], ACT.Tanh, bias=b2c[:, :]).then_inc(delta_ready, 1)
                    if has(g):
                        eng.wait_ge(z_ready, g + 1)
                        eng.activation(z[r][:, :], z[r][:, :], ACT.Gelu).then_inc(gelu_ready, 1)
                over_groups(eng, step, RING, 2)

            @block.tensor
            def _(eng):
                def step(g, r, n):
                    if has(g):
                        w = [eng.value_load(wins[0:1, bass.ds(g * SG + k, 1)], min_val=0, max_val=NT) for k in range(SG)]
                        wait(eng, z_ready, g - 2)
                        eng.wait_ge(hot_ready, g + 1)
                        for k in range(SG):
                            for part in range(3):
                                ins = eng.matmul(bank(2 * r, 2)[:, k * D:(k + 1) * D], hot[r][:, k * P:(k + 1) * P],
                                                 qw[:, bass.ds(w[k] * (3 * D) + part * D, D)], start=part == 0, stop=part == 2)
                        ins.then_inc(qr_ready, 1)
                    if has(g - 1):
                        q = (r - 1) % RING
                        wait(eng, summed, (g - 1) * SG)
                        eng.wait_ge(place_ready, g)
                        for k in range(SG):
                            at = bank(6, 2)[:, k * 256:(k + 1) * 256]
                            to = place[q][:, k * P:k * P + WIN]
                            for hf in range(2):
                                eng.matmul(at[:, hf * WIN:(hf + 1) * WIN],
                                           gath[q][:, k * 2 * D + D + hf * P:k * 2 * D + D + hf * P + P], to, start=True, stop=True)
                            ins = eng.matmul(at[:, 2 * WIN:2 * WIN + TY], place[q][:, k * P:(k + 1) * P],
                                             types[q][:, k * TY:(k + 1) * TY], start=True, stop=True)
                        ins.then_inc(sums_ready, 1)
                over_groups(eng, step, RING, 2)

            @block.vector
            def _(eng):
                for r in range(RING):
                    eng.memset(place[r][:, :], 0.0)
                eng.memset(acc[:, :], 0.0).then_inc(zeroed, 1)
                eng.wait_ge(zeroed, 1)

                def step(g, r, n):
                    q = (r - 1) % RING
                    if has(g - 2):
                        w = [eng.value_load(wins[0:1, bass.ds((g - 2) * SG + k, 1)], min_val=0, max_val=NT) for k in range(SG)]
                    if has(g):
                        eng.wait_ge(key_in[r], (n + 1) * 32)
                        wait(eng, qr_ready, g - 2)
                        eng.tensor_scalar(hot[r][:, :], key[r][:, :], pcol[:, 0:1], None, ALU.is_equal).then_inc(hot_ready, 1)
                    if has(g - 2):
                        eng.wait_ge(sums_ready, g - 1)
                        for k in range(SG):
                            to = acc[:, bass.ds(w[k] * ACW1, ACW1)]
                            wait(eng, summed, (g - 2) * SG + k)
                            eng.tensor_tensor(to, bank(6, 2)[:, k * 256:k * 256 + ACW1], to, ALU.add).then_inc(summed, 1)
                    if has(g - 1):
                        eng.wait_ge(gelu_ready, g)
                        for k in range(SG):
                            zk = z[q][:, k * D:(k + 1) * D]
                            ins = eng.tensor_tensor_reduce(zk, zk, w2b[:, :], 1.0, 0.0, ALU.mult, ALU.add, logit[q][:, k:k + 1])
                        ins.then_inc(logit_ready, 1)
                    if has(g):
                        wait(eng, logit_ready, g - 2)
                        eng.wait_ge(got[r], (n + 1) * (16 * SG))
                        eng.wait_ge(qr_ready, g + 1)
                        eng.tensor_tensor(z[r][:, :].rearrange("p (k d) -> p k d", k=SG),
                                          bank(2 * r, 2).rearrange("p (k d) -> p k d", k=SG),
                                          gath[r][:, :].rearrange("p (k d) -> p k d", k=SG)[:, :, 0:D], ALU.add).then_inc(z_ready, 1)
                    if has(g - 1):
                        eng.wait_ge(cur_ready, g)
                        eng.tensor_tensor(types[q][:, :].rearrange("p (k t) -> p k t", k=SG), bc(iof[:, 0:TY], SG),
                                          bi(curf[q][:, 0:SG], TY), ALU.is_equal)
                        eng.wait_ge(delta_ready, g)
                        eng.tensor_scalar(ew[q][:, :], delta[q][:, :], esc[:, 0:1], 1.0, ALU.mult, ALU.add).then_inc(ew_ready, 1)
                        eng.wait_ge(ew_ready, g)
                        for k in range(SG):
                            ins = eng.tensor_scalar(place[q][:, k * P:k * P + WIN], iof[:, 0:WIN], curf[q][:, SG + k:SG + k + 1],
                                                    ew[q][:, k:k + 1], ALU.is_equal, ALU.mult)
                        ins.then_inc(place_ready, 1)
                over_groups(eng, step, RING, 2)

        b5 = ExitStack()
        with b5:
            def s(name, shape, dt):
                return sbt(name, shape, dt, b5)

            def sem(name):
                return b5.enter_context(nc.semaphore(name))

            deg = s("deg", [WIN, NT], fp32)
            rd = s("rd", [WIN, NT], fp32)
            sums = s("sums", [P, GN * ACW1], fp32)
            tt = s("tt", [TY, GN * WIN], fp32)
            ge = s("ge", [WIN, GN * D], fp32)
            gT = s("gT", [P, GN * 2 * WIN], fp32)
            h1 = [s(f"h1_{r}", [WIN, GN * D], fp32) for r in range(2)]
            upb2 = s("upb2", [WIN, D], fp32)
            lng = s("lng", [WIN, D], fp32)
            lnb = s("lnb", [WIN, D], fp32)
            st = s("st_c", [WIN, GN * 6], fp32)
            mv = s("mv_c", [WIN, GN * 2], fp32)
            mva = s("mva", [WIN, NT * 2], fp32)
            sd = s("sd_c", [WIN, NT], fp32)
            rs = s("rs_c", [WIN, NT], fp32)
            nb = s("nb_c", [WIN, NT], fp32)
            yn = [s(f"yn{r}", [WIN, GN * D], fp32) for r in range(2)]
            mva3 = mva[:, :].rearrange("p (t c) -> p t c", c=2)
            consts_in = sem("consts_in")
            h1_in = sem("h1_in")
            sums_at = sem("sums_at")
            tt_ready = sem("tt_ready")
            tt_out = sem("tt_out")
            b_ready = sem("b_ready")
            rd_ready = sem("rd_ready")
            uc_ready = sem("uc_ready")
            u_ready = sem("u_ready")
            ge_ready = sem("ge_ready")
            g_ready = sem("g_ready")
            gT_ready = sem("gT_ready")
            y_ps = sem("y_ps")
            y_ready = sem("y_ready")
            bn = sem("bn_c")
            ln = sem("ln_c")
            sd_ready = sem("sd_ready_c")
            hb_ready = sem("hb_ready")
            yn_ready = sem("yn_ready")
            gained = sem("gained")
            xb_ready = sem("xb_ready_c")
            out_ready = sem("out_ready")
            stored = sem("stored")
            hop_a = sem("hop_a_c")
            hop_v = sem("hop_v_c")
            hop_p = sem("hop_p_c")
            hop_s = sem("hop_s_c")
            block = b5.enter_context(nc.Block())

            @block.sync
            def _(eng):
                for t, name in ((upb2, "L1_gnn_up_b2"), (lng, "L1_gnn_ln_g"), (lnb, "L1_gnn_ln_b")):
                    eng.dma_start(t[:, :], prow(A[name], WIN)).then_inc(consts_in, 16)

                def load(i):
                    wait(eng, y_ready, i)
                    eng.sem_inc(hop_s, 1)
                    eng.dma_start(h1[0][:, :].rearrange("p (k d) -> p k d", k=GN),
                                  ph_d[bass.ds(i * (GN * WIN), GN * WIN), D:2 * D].rearrange("(k p) d -> p k d", p=WIN))\
                       .then_inc(h1_in, 16)
                over_tiles(eng, load, 0)

                def store(i):
                    eng.wait_ge(out_ready, i + 1)
                    eng.sem_inc(hop_s, 1)
                    eng.dma_start(out[bass.ds(i * (GN * WIN), GN * WIN), :].rearrange("(k p) d -> p k d", p=WIN),
                                  x3[:, bass.ds(i * GN, GN), :]).then_inc(stored, 16)
                with eng.Fori(0, NG - 1) as i:
                    store(i)
                eng.wait_ge(out_ready, NG)
                full = (NT - 1) * WIN
                eng.dma_start(out[(NG - 1) * GN * WIN:full, :].rearrange("(k p) d -> p k d", p=WIN),
                              x3[:, (NG - 1) * GN:NT - 1, :]).then_inc(stored, 16)
                eng.dma_start(out[full:N, :], x3[0:LAST, NT - 1, :]).then_inc(stored, 16)
                eng.wait_ge(stored, 16 * (NG + 1))

            @block.gpsimd
            def _(eng):
                eng.wait_ge(consts_in, 48)

                def step(i):
                    wait(eng, b_ready, i)
                    eng.sem_inc(hop_p, 1)
                    eng.tensor_copy(sums[:, :], acc[:, bass.ds(i * (GN * ACW1), GN * ACW1)]).then_inc(sums_at, 1)
                    ug = up[:, bass.ds(i * (GN * D), GN * D)].rearrange("p (k d) -> p k d", k=GN)
                    eng.tensor_tensor(ug, ug, bc(c2[:, :], GN), ALU.add).then_inc(uc_ready, 1)
                    eng.wait_ge(h1_in, i * 16 + 16)
                    hg = h1[0][:, :].rearrange("p (k d) -> p k d", k=GN)
                    eng.tensor_tensor(hg, hg, bc(upb2[:, :], GN), ALU.add).then_inc(hb_ready, 1)
                    xg = x3[:, bass.ds(i * GN, GN), :]
                    eng.tensor_tensor(xg, xg, bc(lnb[:, :], GN), ALU.add).then_inc(xb_ready, 1)
                over_tiles(eng, step, 0)

            @block.tensor
            def _(eng):
                def step(i):
                    eng.wait_ge(sums_at, i + 1)
                    for k in range(GN):
                        ins = eng.transpose(bank(0)[0:TY, k * WIN:(k + 1) * WIN],
                                            sums[0:WIN, k * ACW1 + 2 * WIN:k * ACW1 + ACW1], ident[0:WIN, 0:WIN])
                    ins.then_inc(tt_ready, 1)
                    wait(eng, u_ready, i)
                    eng.wait_ge(tt_out, i + 1)
                    for k in range(GN):
                        at = bank(2, 2)[0:WIN, k * D:(k + 1) * D]
                        for hf in range(2):
                            eng.matmul(at, sums[:, k * ACW1 + hf * WIN:k * ACW1 + (hf + 1) * WIN], mc[:, hf * D:(hf + 1) * D],
                                       start=hf == 0, stop=False)
                        ins = eng.matmul(at, tt[:, k * WIN:(k + 1) * WIN], em[:, :], start=False, stop=True)
                    ins.then_inc(b_ready, 1)
                    eng.wait_ge(ge_ready, i + 1)
                    for k in range(GN):
                        for hf in range(2):
                            ins = eng.transpose(bank(4, 2)[:, k * 256 + hf * WIN:k * 256 + (hf + 1) * WIN],
                                                ge[:, k * D + hf * P:k * D + hf * P + P], ident[0:WIN, 0:WIN])
                    ins.then_inc(g_ready, 1)
                    eng.wait_ge(gT_ready, i + 1)
                    for k in range(GN):
                        for hf in range(2):
                            ins = eng.matmul(bank(6, 2)[0:WIN, k * D:(k + 1) * D], gT[:, (k * 2 + hf) * WIN:(k * 2 + hf + 1) * WIN],
                                             upw2[:, hf * D:(hf + 1) * D], start=hf == 0, stop=hf == 1)
                    ins.then_inc(y_ps, 1)
                over_tiles(eng, step, 0)

            @block.scalar
            def _(eng):
                def step(i):
                    eng.wait_ge(u_ready, i + 1)
                    eng.sem_inc(hop_a, 1)
                    eng.activation(ge[:, :], up[:, bass.ds(i * (GN * D), GN * D)], ACT.Gelu).then_inc(ge_ready, 1)
                over_tiles(eng, step, 0)
                eng.wait_ge(ln, 1)
                eng.activation(sd[:, :], mva3[:, :, 1], ACT.Sqrt).then_inc(sd_ready, 1)
                eng.wait_ge(ln, 3)

                def norm(i):
                    wait(eng, gained, i)
                    eng.sem_inc(hop_a, 1)
                    for k in range(GN):
                        t = i * GN + k
                        ins = eng.activation(yn[0][:, k * D:(k + 1) * D], up[:, bass.ds(t * D, D)], ACT.Identity,
                                             scale=rs[:, bass.ds(t, 1)], bias=nb[:, bass.ds(t, 1)])
                    ins.then_inc(yn_ready, 1)
                over_tiles(eng, norm, 0)

            @block.vector
            def _(eng):
                a4 = acc[0:WIN, 0:NT * ACW1].rearrange("p (w c) -> p w c", c=ACW1)[:, :, 2 * WIN:ACW1]
                eng.tensor_reduce(deg[:, :], a4, AX.X, ALU.add).then_inc(rd_ready, 1)
                eng.wait_ge(rd_ready, 1)
                eng.tensor_scalar(deg[:, :], deg[:, :], 1.0, None, ALU.max).then_inc(rd_ready, 1)
                eng.wait_ge(rd_ready, 2)
                eng.reciprocal(rd[:, :], deg[:, :]).then_inc(rd_ready, 1)
                eng.wait_ge(rd_ready, 3)
                st3 = st[:, :].rearrange("p (k c) -> p k c", k=GN)
                mv3 = mv[:, :].rearrange("p (k c) -> p k c", k=GN)

                def step(i):
                    eng.wait_ge(tt_ready, i + 1)
                    eng.tensor_copy(tt[:, :], bank(0)[0:TY, 0:GN * WIN]).then_inc(tt_out, 1)
                    eng.wait_ge(uc_ready, i + 1)
                    eng.wait_ge(b_ready, i + 1)
                    for k in range(GN):
                        t = i * GN + k
                        ut = up[:, bass.ds(t * D, D)]
                        ins = eng.scalar_tensor_tensor(out=ut, in0=bank(2, 2)[0:WIN, k * D:(k + 1) * D], scalar=rd[:, bass.ds(t, 1)],
                                                       in1=ut, op0=ALU.mult, op1=ALU.add)
                    ins.then_inc(u_ready, 1)
                    eng.wait_ge(g_ready, i + 1)
                    eng.sem_inc(hop_v, 1)
                    eng.tensor_copy(gT[:, :].rearrange("p (k c) -> p k c", k=GN),
                                    bank(4, 2).rearrange("p (k c) -> p k c", k=GN)[:, :, 0:2 * WIN]).then_inc(gT_ready, 1)
                    eng.wait_ge(hb_ready, i + 1)
                    eng.wait_ge(y_ps, i + 1)
                    yg = up[:, bass.ds(i * (GN * D), GN * D)]
                    eng.tensor_tensor(yg, bank(6, 2)[0:WIN, :], h1[0][:, :], ALU.add).then_inc(y_ready, 1)
                    eng.wait_ge(y_ready, i + 1)
                    eng.sem_inc(hop_v, 1)
                    for k in range(GN):
                        ins = eng.bn_stats(st3[:, k, :], up[:, bass.ds((i * GN + k) * D, D)])
                    ins.then_inc(bn, 1)
                    eng.wait_ge(bn, i * 3 + 1)
                    eng.sem_inc(hop_v, 1)
                    for k in range(GN):
                        ins = eng.bn_aggr(mv3[:, k, :], st3[:, k, :])
                    ins.then_inc(bn, 1)
                    eng.wait_ge(bn, i * 3 + 2)
                    eng.sem_inc(hop_v, 1)
                    eng.tensor_copy(mva[:, bass.ds(i * (GN * 2), GN * 2)], mv[:, :]).then_inc(bn, 1)
                over_tiles(eng, step, 0)
                eng.wait_ge(bn, NG * 3)
                eng.tensor_scalar(mva3[:, :, 1], mva3[:, :, 1], 1e-5, None, ALU.add).then_inc(ln, 1)
                eng.wait_ge(sd_ready, 1)
                eng.reciprocal(rs[:, :], sd[:, :]).then_inc(ln, 1)
                eng.wait_ge(ln, 2)
                eng.scalar_tensor_tensor(out=nb[:, :], in0=mva3[:, :, 0], scalar=-1.0, in1=rs[:, :],
                                         op0=ALU.mult, op1=ALU.mult).then_inc(ln, 1)

                def put(i):
                    eng.wait_ge(yn_ready, i + 1)
                    eng.wait_ge(consts_in, 48)
                    wait(eng, out_ready, i)
                    yg = yn[0][:, :].rearrange("p (k d) -> p k d", k=GN)
                    eng.tensor_tensor(yn[1][:, :].rearrange("p (k d) -> p k d", k=GN), yg, bc(lng[:, :], GN), ALU.mult).then_inc(gained, 1)
                    eng.wait_ge(xb_ready, i + 1)
                    eng.wait_ge(gained, i + 1)
                    xg = x[:, bass.ds(i * (GN * D), GN * D)]
                    eng.tensor_tensor(xg, yn[1][:, :], xg, ALU.add).then_inc(out_ready, 1)
                over_tiles(eng, put, 0)


_OUTS = [((3125, 256), 'float32')]


def kernel(**inputs):
    import numpy as _np
    import concourse.bacc as _bacc
    from concourse import mybir as _mybir
    from concourse.bass_utils import run_bass_kernel_spmd as _run

    nc = _bacc.Bacc("TRN2", target_bir_lowering=False, num_devices=1)
    arrays, args = {}, {}
    for name in inputs:
        a = _np.ascontiguousarray(inputs[name])
        arrays[f"in_{name}_dram"] = a
        args[name] = nc.dram_tensor(f"in_{name}_dram", a.shape, _mybir.dt.from_np(a.dtype), kind="ExternalInput").ap()
    outs = []
    for i, (shape, dtype) in enumerate(_OUTS):
        dt = _mybir.dt.from_np(_np.dtype(dtype))
        outs.append(nc.dram_tensor(f"out_{i}_dram", shape, dt, kind="ExternalOutput").ap())
    gnn_two_layers(nc, args, outs[0])
    r = _run(nc, [arrays], core_ids=[0])
    return r.results[0]["out_0_dram"]
```

```python
import concourse.bass as bass
from concourse import mybir
from contextlib import ExitStack
from itertools import count


def gnn_two_layers(nc, A, out):
    fp32, bf16, i32 = mybir.dt.float32, mybir.dt.bfloat16, mybir.dt.int32
    ALU, ACT, AX = mybir.AluOpType, mybir.ActivationFunctionType, mybir.AxisListType

    P = 128
    N, D = A["x"].shape
    E = A["src"].shape[0]
    TY = A["L1_gnn_edge_emb"].shape[0]
    WIN = P - TY
    NT = -(-N // WIN)
    LAST = N - (NT - 1) * WIN
    GN = 4
    NG = NT // GN
    assert NG * GN == NT and D == 2 * P
    ROW = 512
    ER = -(-E // ROW)
    EL = E - (ER - 1) * ROW
    BLK = 32
    FLD = 5
    NB = ER * ROW // BLK
    SG = 4
    RB = P // BLK
    SLOTS = (E + NT * (BLK - 1 + P - 1)) // P
    NGR = -(-SLOTS // SG)
    SLOTS = NGR * SG
    assert NGR % 2 == 1 and NGR % 3 == 2 and NGR <= P
    RC = -(-SLOTS * RB // P)
    NPAD = 4000.0
    NEG = 3.0e38
    GW = SG * P

    blocks_d = nc.dram_tensor("blocks_d", [NB + 1, FLD * BLK], fp32, kind="Internal").ap()
    want_d = nc.dram_tensor("want_d", [RC * P], i32, kind="Internal").ap()
    rec_d = nc.dram_tensor("rec_d", [RC * P, FLD * BLK], fp32, kind="Internal").ap()
    win_d = nc.dram_tensor("win_d", [SLOTS], i32, kind="Internal").ap()
    node_row_d = nc.dram_tensor("node_row_d", [SLOTS * P], bf16, kind="Internal").ap()
    type_row_d = nc.dram_tensor("type_row_d", [SLOTS * P], bf16, kind="Internal").ap()
    start_row_d = nc.dram_tensor("start_row_d", [SLOTS * P], bf16, kind="Internal").ap()
    hp_d = nc.dram_tensor("hp_d", [NT * WIN, D], fp32, kind="Internal").ap()
    ph_d = nc.dram_tensor("ph_d", [NT * WIN, 2 * D], fp32, kind="Internal").ap()

    def bc(ap2, m):
        p, n = ap2.shape
        return ap2.rearrange("p (a n) -> p a n", a=1).to_broadcast([p, m, n])

    def bi(ap2, m):
        p, n = ap2.shape
        return ap2.rearrange("p (n a) -> p n a", a=1).to_broadcast([p, n, m])

    def prow(ap1, p):
        return ap1.rearrange("(a n) -> a n", a=1).to_broadcast([p, ap1.shape[0]])

    top = ExitStack()
    with top:
        def sbt(name, shape, dt, ctx=top):
            return ctx.enter_context(nc.sbuf_tensor(name, shape, dt))

        ps = top.enter_context(nc.psum_tensor("ps", [P, 8 * 512], fp32))
        x = sbt("x_sb", [WIN, NT * D], fp32)
        acc = sbt("acc", [P, (NT + 1) * 2 * P], fp32)
        ident = sbt("ident", [P, P], fp32)
        iof = sbt("iof", [P, P], fp32)
        pcol = sbt("pcol", [P, 1], fp32)
        srcs = sbt("srcs", [P, NGR * SG], i32)
        edgef = sbt("edgef", [P, NGR * 4 * SG], fp32)
        wins = sbt("wins", [1, SLOTS], i32)
        wn = sbt("wn", [P, 2 * D], fp32)
        ACW0 = 2 * WIN
        ACW1 = 2 * WIN + TY
        x3 = x[:, :].rearrange("p (t d) -> p t d", t=NT)
        edgef4 = edgef[:, :].rearrange("p (g f k) -> p g f k", g=NGR, f=4)

        def bank(b, n=1):
            return ps[:, b * 512:(b + n) * 512]

        b1 = ExitStack()
        with b1:
            def s(name, shape, dt):
                return sbt(name, shape, dt, b1)

            def sem(name):
                return b1.enter_context(nc.semaphore(name))

            wraw = s("wraw", [P, 3 * 2 * D], fp32)
            wpT = s("wpT", [P, 2 * D], fp32)
            wsT = s("wsT", [P, 2 * D], fp32)
            bpool = s("bpool", [WIN, D], fp32)
            bself = s("bself", [WIN, D], fp32)
            bneigh = s("bneigh", [WIN, D], fp32)
            nat_i = s("nat_i", [ER, 4 * ROW], i32)
            nat_w = s("nat_w", [ER, ROW], fp32)
            nat_f = s("nat_f", [ER, 2 * ROW], fp32)
            same = s("same", [ER, ROW], fp32)
            blk = s("blk", [ER, ROW * FLD], fp32)
            blk4 = blk[:, :].rearrange("p (b f e) -> p b f e", f=FLD, e=BLK)
            padb = s("padb", [1, FLD * BLK], fp32)
            junk = s("junk", [P, 4 * ROW], fp32)
            cnt = s("cnt", [ER, NT + 1], fp32)
            ones = s("ones", [P, P], fp32)
            io_i = s("io_i", [P, P], i32)
            pc_i = s("pc_i", [P, 1], i32)
            j_i = s("j_i", [NGR, SG], i32)
            r_i = s("r_i", [NGR, SG * RB], i32)
            jf = s("jf", [NGR, SG], fp32)
            rf = s("rf", [NGR, SG * RB], fp32)
            s_f = s("s_f", [NGR, NT + 1], fp32)
            s_i = s("s_i", [NGR, NT + 1], i32)
            fb_i = s("fb_i", [NGR, NT + 1], i32)
            fb = s("fb", [NGR, NT + 1], fp32)
            nsl = s("nsl", [NGR, NT], fp32)
            nsl_i = s("nsl_i", [NGR, NT], i32)
            zero = s("zero", [NGR, NT], fp32)
            cum = s("cum", [NGR, NT], fp32)
            wf = s("wf", [NGR, SG], fp32)
            w_i = s("w_i", [NGR, SG], i32)
            w0 = s("w0", [NGR, SG], fp32)
            cp = s("cp", [NGR, SG], fp32)
            sb0 = s("sb0", [NGR, SG], fp32)
            wantf = s("wantf", [NGR, SG * RB], fp32)
            want_i = s("want_i", [NGR, SG * RB], i32)
            want_pad = s("want_pad", [1, RC * P - SLOTS * RB], i32)
            want = s("want", [P, RC], i32)
            recs = s("recs", [P, RC * FLD * BLK], fp32)
            nat = s("nat", [NGR, SG * RB * FLD * BLK], fp32)
            nat4 = nat[:, :].rearrange("p (b f e) -> p b f e", f=FLD, e=BLK)
            prev = s("prev", [NGR, 1], fp32)
            dsts = s("dsts", [NGR, GW + 1], fp32)
            flds = s("flds", [NGR, FLD * GW], fp32)
            flds3 = flds[:, :].rearrange("p (f e) -> p f e", f=FLD)
            row_n = s("row_n", [NGR, GW], bf16)
            row_t = s("row_t", [NGR, GW], bf16)
            row_s = s("row_s", [NGR, GW], bf16)
            eqp = s("eqp", [NGR, GW], fp32)
            st = s("st", [WIN, GN * 6], fp32)
            mv = s("mv", [WIN, GN * 2], fp32)
            ve = s("ve", [WIN, GN], fp32)
            sd = s("sd", [WIN, GN], fp32)
            rs = s("rs", [WIN, GN], fp32)
            nb = s("nb", [WIN, GN], fp32)
            h = s("h", [WIN, GN * D], fp32)
            hT = s("hT", [P, GN * 2 * WIN], fp32)
            hpb = s("hpb", [WIN, GN * D], fp32)
            hpo = s("hpo", [WIN, GN * D], fp32)
            st3 = st[:, :].rearrange("p (k c) -> p k c", k=GN)
            mv3 = mv[:, :].rearrange("p (k c) -> p k c", k=GN)

            pads_set = sem("pads_set")
            x_pad = sem("x_pad")
            edges_in = sem("edges_in")
            x_in = sem("x_in")
            w_in = sem("w_in")
            bias_in = sem("bias_in")
            io_set = sem("io_set")
            id_set = sem("id_set")
            prep = sem("prep")
            blk_ready = sem("blk_ready")
            blk_out = sem("blk_out")
            cnt_ready = sem("cnt_ready")
            starts_ready = sem("starts_ready")
            starts_read = sem("starts_read")
            want_ready = sem("want_ready")
            want_out = sem("want_out")
            want_in = sem("want_in")
            recs_in = sem("recs_in")
            recs_out = sem("recs_out")
            nat_in = sem("nat_in")
            rows_ready = sem("rows_ready")
            rows_out = sem("rows_out")
            flds_ready = sem("flds_ready")
            cols_ready = sem("cols_ready")
            wT_ps = sem("wT_ps")
            wT_ready = sem("wT_ready")
            bn = sem("bn")
            var_ready = sem("var_ready")
            sd_ready = sem("sd_ready")
            nb_ready = sem("nb_ready")
            rs_ready = sem("rs_ready")
            h_ready = sem("h_ready")
            t_ready = sem("t_ready")
            hT_ready = sem("hT_ready")
            mm_ready = sem("mm_ready")
            bsum_ready = sem("bsum_ready")
            xb_ready = sem("xb_ready")
            evac = sem("evac")
            hpb_free = sem("hpb_free")
            hpo_ready = sem("hpo_ready")
            hpo_out = sem("hpo_out")
            hpo_free = sem("hpo_free")
            hop_v = sem("hop_v")
            hop_a = sem("hop_a")
            hop_p = sem("hop_p")
            block = b1.enter_context(nc.Block())

            @block.sync
            def _(eng):
                eng.wait_ge(pads_set, 1)
                full = (ER - 1) * ROW
                for f, name, off in ((1, "dst", 0), (3, "dst", 1), (0, "src", 0), (2, "edge_type_16", 0)):
                    dst_cols = slice(f * ROW, (f + 1) * ROW)
                    eng.dma_start(nat_i[0:ER - 1, dst_cols],
                                  A[name][off:off + full].rearrange("(p e) -> p e", e=ROW)).then_inc(edges_in, 16)
                    eng.dma_start(nat_i[ER - 1:ER, f * ROW:f * ROW + EL - off],
                                  A[name][off + full:E].rearrange("(p e) -> p e", p=1)).then_inc(edges_in, 16)
                w1 = A["edge_weight1"].rearrange("e o -> (e o)")
                eng.dma_start(nat_w[0:ER - 1, :], w1[0:full].rearrange("(p e) -> p e", e=ROW)).then_inc(edges_in, 16)
                eng.dma_start(nat_w[ER - 1:ER, 0:EL], w1[full:E].rearrange("(p e) -> p e", p=1)).then_inc(edges_in, 16)
                for n, name in enumerate(("L0_gnn_W_pool", "L0_gnn_W_self", "L0_gnn_W_neigh")):
                    eng.dma_start(wraw[:, n * 2 * D:(n + 1) * 2 * D].rearrange("p (o i) -> p o i", o=2),
                                  A[name].rearrange("(o p) i -> p o i", p=P)).then_inc(w_in, 16)
                eng.dma_start(bpool[:, :], prow(A["L0_gnn_b_pool"], WIN)).then_inc(bias_in, 16)
                eng.dma_start(bself[:, :], prow(A["L0_gnn_b_self"], WIN)).then_inc(bias_in, 16)
                eng.dma_start(bneigh[:, :], prow(A["L0_gnn_b_neigh"], WIN)).then_inc(bias_in, 16)
                eng.wait_ge(blk_ready, 2)
                eng.dma_start(blocks_d[0:NB, :].rearrange("(p b) f -> p (b f)", p=ER), blk[:, :]).then_inc(blk_out, 16)
                eng.dma_start(blocks_d[NB:NB + 1, :], padb[:, :]).then_inc(blk_out, 16)
                eng.wait_ge(want_ready, 1)
                eng.dma_start(want_d[0:SLOTS * RB].rearrange("(p c) -> p c", p=NGR), want_i[:, :]).then_inc(want_out, 16)
                eng.dma_start(want_d[SLOTS * RB:RC * P].rearrange("(p c) -> p c", p=1), want_pad[:, :]).then_inc(want_out, 16)
                eng.dma_start(win_d.rearrange("(p c) -> p c", p=NGR), w_i[:, :]).then_inc(want_out, 16)
                eng.wait_ge(want_out, 48)
                with nc.allow_non_contiguous_dma(reason="a small table of indices turned over"):
                    eng.dma_start(want[:, :], want_d.rearrange("(c p) -> p c", p=P)).then_inc(want_in, 16)
                eng.dma_start(wins[:, :], win_d.rearrange("(a c) -> a c", a=1)).then_inc(want_in, 16)
                eng.wait_ge(recs_in, 16 * RC)
                eng.dma_start(rec_d.rearrange("(c p) f -> p c f", p=P),
                              recs[:, :].rearrange("p (c f) -> p c f", c=RC)).then_inc(recs_out, 16)
                eng.wait_ge(recs_out, 16)
                eng.dma_start(nat[:, :], rec_d[0:SLOTS * RB, :].rearrange("(g b) f -> g (b f)", g=NGR)).then_inc(nat_in, 16)
                last_dst = 1 * BLK + BLK - 1
                per = SG * RB * FLD * BLK
                flat = rec_d.rearrange("r f -> (r f)")
                first = (SG * RB - 1) * FLD * BLK + last_dst
                with nc.allow_non_contiguous_dma(reason="one element of each group"):
                    eng.dma_start(prev[1:NGR, :],
                                  flat[0:(NGR - 1) * per].rearrange("(g c) -> g c", c=per)[:, first:first + 1])\
                       .then_inc(nat_in, 16)
                eng.wait_ge(rows_ready, 3)
                for d, t in ((node_row_d, row_n), (type_row_d, row_t), (start_row_d, row_s)):
                    eng.dma_start(d.rearrange("(g e) -> g e", g=NGR), t[:, :]).then_inc(rows_out, 16)
                eng.wait_ge(rows_out, 48)

            @block.scalar
            def _(eng):
                eng.wait_ge(x_pad, 1)
                eng.dma_start(x3[:, 0:NT - 1, :], A["x"][0:(NT - 1) * WIN, :].rearrange("(t p) d -> p t d", p=WIN)).then_inc(x_in, 16)
                eng.dma_start(x3[0:LAST, NT - 1, :], A["x"][(NT - 1) * WIN:N, :]).then_inc(x_in, 16)
                for n, w in enumerate((wpT, wsT, wn)):
                    eng.wait_ge(wT_ps, n + 1)
                    eng.activation(w[:, :], bank(n), ACT.Copy).then_inc(wT_ready, 1)
                eng.sem_inc(hpb_free, 1)

                def h0(i):
                    eng.wait_ge(var_ready, i + 1)
                    eng.activation(sd[:, :], ve[:, :], ACT.Sqrt).then_inc(sd_ready, 1)
                    eng.wait_ge(nb_ready, i + 1)
                    eng.sem_inc(hop_a, 1)
                    for k in range(GN):
                        ins = eng.activation(h[:, k * D:(k + 1) * D], x[:, bass.ds((i * GN + k) * D, D)], ACT.Relu,
                                             scale=rs[:, k:k + 1], bias=nb[:, k:k + 1])
                    ins.then_inc(h_ready, 1)

                def relu(i):
                    eng.wait_ge(evac, 2 * i + 1)
                    eng.wait_ge(hpo_free, i + 1)
                    eng.activation(hpo[:, :], hpb[:, :], ACT.Relu).then_inc(hpo_ready, 1)

                h0(0)
                with eng.Fori(0, NG - 1) as i:
                    h0(i + 1)
                    relu(i)
                    eng.wait_ge(hpo_ready, i + 1)
                    eng.sem_inc(hpb_free, 1)
                relu(NG - 1)

            @block.gpsimd
            def _(eng):
                eng.memset(ident[:, :], 0.0).then_inc(id_set, 1)
                eng.wait_ge(id_set, 1)
                eng.affine_select(out=ident[:, :], in_=ident[:, :], compare_op=ALU.not_equal, fill=1.0,
                                  base=0, pattern=[[-1, P]], channel_multiplier=1).then_inc(id_set, 1)
                eng.iota(io_i[:, :], [[1, P]], base=0, channel_multiplier=0).then_inc(io_set, 1)
                eng.iota(pc_i[:, :], [[0, 1]], base=0, channel_multiplier=1).then_inc(io_set, 1)
                eng.iota(j_i[:, :], [[1, SG]], base=0, channel_multiplier=SG).then_inc(io_set, 1)
                eng.iota(r_i[:, :], [[0, SG], [1, RB]], base=0, channel_multiplier=0).then_inc(io_set, 1)
                eng.wait_ge(bias_in, 48)
                eng.tensor_tensor(bself[:, :], bself[:, :], bneigh[:, :], ALU.add).then_inc(bsum_ready, 1)
                eng.wait_ge(want_in, 32)
                eng.wait_ge(blk_out, 32)
                for c in range(RC):
                    eng.indirect_dma_start(recs[:, c * FLD * BLK:(c + 1) * FLD * BLK], None, blocks_d[:, :],
                                           bass.IndirectOffsetOnAxis(ap=want[:, c:c + 1], axis=0)).then_inc(recs_in, 16)
                eng.wait_ge(bsum_ready, 1)
                eng.sem_inc(hpo_free, 1)
                with eng.Fori(0, NG) as i:
                    eng.wait_ge(h_ready, i + 1)
                    eng.sem_inc(hop_p, 1)
                    g3 = x[:, bass.ds(i * GN * D, GN * D)].rearrange("p (k d) -> p k d", k=GN)
                    eng.tensor_tensor(g3, g3, bc(bself[:, :], GN), ALU.add).then_inc(xb_ready, 1)
                    eng.wait_ge(hpo_ready, i + 1)
                    eng.sem_inc(hop_p, 1)
                    eng.dma_start(hp_d[bass.ds(i * GN * WIN, GN * WIN), :].rearrange("(k p) d -> p k d", p=WIN),
                                  hpo[:, :].rearrange("p (k d) -> p k d", k=GN)).then_inc(hpo_out, 16)
                    eng.wait_ge(hpo_out, 16 * i + 16)
                    eng.sem_inc(hpo_free, 1)

            @block.tensor
            def _(eng):
                eng.wait_ge(id_set, 2)
                eng.wait_ge(w_in, 48)
                for n in range(3):
                    for kin in range(2):
                        for o in range(2):
                            ins = eng.transpose(bank(n)[:, kin * D + o * P:kin * D + o * P + P],
                                                wraw[:, (n * 2 + o) * D + kin * P:(n * 2 + o) * D + kin * P + P], ident[:, :])
                    ins.then_inc(wT_ps, 1)
                eng.wait_ge(cnt_ready, NT)
                eng.matmul(bank(3)[0:NGR, 0:NT + 1], ones[0:ER, 0:NGR], cnt[:, :], start=True, stop=True).then_inc(starts_ready, 1)
                eng.wait_ge(starts_read, 1)
                eng.wait_ge(wT_ready, 3)
                with eng.Fori(0, NG) as i:
                    eng.wait_ge(h_ready, i + 1)
                    for k in range(GN):
                        for hf in range(2):
                            ins = eng.transpose(bank(0, 2)[:, k * 256 + hf * WIN:k * 256 + (hf + 1) * WIN],
                                                h[:, k * D + hf * P:k * D + hf * P + P], ident[0:WIN, 0:WIN])
                    ins.then_inc(t_ready, 1)
                    eng.wait_ge(hT_ready, i + 1)
                    for k in range(GN):
                        for b, w in ((2, wpT), (4, wsT)):
                            for hf in range(2):
                                ins = eng.matmul(bank(b, 2)[0:WIN, k * D:(k + 1) * D],
                                                 hT[:, (k * 2 + hf) * WIN:(k * 2 + hf + 1) * WIN],
                                                 w[:, hf * D:(hf + 1) * D], start=hf == 0, stop=hf == 1)
                    ins.then_inc(mm_ready, 1)
                eng.wait_ge(flds_ready, 1)
                eng.wait_ge(evac, 2 * NG)
                for f in range(FLD):
                    for k in range(SG):
                        ins = eng.transpose(bank(f)[:, k * NGR:(k + 1) * NGR],
                                            flds[:, f * GW + k * P:f * GW + (k + 1) * P], ident[0:NGR, 0:NGR])
                    ins.then_inc(cols_ready, 1)

            @block.vector
            def _(eng):
                eng.memset(nat_i[:, :].rearrange("p (f e) -> p f e", f=4)[:, 0:3:2, :], 0)
                eng.memset(nat_i[:, :].rearrange("p (f e) -> p f e", f=4)[:, 1:4:2, :], int(NPAD))
                eng.memset(nat_w[:, :], 0.0).then_inc(pads_set, 1)
                eng.memset(x[:, (NT - 1) * D:NT * D], 0.0).then_inc(x_pad, 1)
                eng.memset(cnt[:, :], 0.0)
                eng.memset(ones[:, :], 1.0)
                eng.memset(zero[:, :], 0.0)
                eng.memset(padb[:, 0:BLK], 0.0)
                eng.memset(padb[:, BLK:2 * BLK], NPAD)
                eng.memset(padb[:, 2 * BLK:4 * BLK], 0.0)
                eng.memset(padb[:, 4 * BLK:5 * BLK], -NPAD).then_inc(blk_ready, 1)
                eng.memset(want_pad[:, :], NB)
                step = count(1)
                eng.memset(prev[:, :], -1.0).then_inc(prep, 1)
                eng.wait_ge(prep, next(step))
                eng.wait_ge(io_set, 4)
                eng.tensor_copy(iof[:, :], io_i[:, :])
                eng.tensor_copy(pcol[:, :], pc_i[:, :])
                eng.tensor_copy(jf[:, :], j_i[:, :])
                eng.tensor_copy(rf[:, :], r_i[:, :]).then_inc(prep, 1)
                eng.wait_ge(prep, next(step))
                eng.tensor_scalar(zero[:, 0:1], pcol[0:NGR, :], 0.0, None, ALU.mult)
                eng.tensor_scalar(junk[:, 0:1], pcol[:, :], float(WIN), float(-WIN), ALU.is_ge, ALU.mult).then_inc(prep, 1)
                eng.wait_ge(prep, next(step))
                eng.tensor_tensor(pcol[:, :], pcol[:, :], junk[:, 0:1], ALU.add).then_inc(prep, 1)
                eng.wait_ge(prep, next(step))
                eng.wait_ge(edges_in, 160)
                ni = nat_i[:, :].rearrange("p (f e) -> p f e", f=4)
                eng.tensor_copy(nat_f[:, 0:ROW], ni[:, 1, :])
                eng.tensor_copy(nat_f[:, ROW:2 * ROW], ni[:, 3, :]).then_inc(prep, 1)
                eng.wait_ge(prep, next(step))
                def be(ap):
                    return ap.rearrange("p (b e) -> p b e", e=BLK)
                eng.tensor_tensor(same[:, :], nat_f[:, 0:ROW], nat_f[:, ROW:2 * ROW], ALU.is_equal).then_inc(prep, 1)
                eng.tensor_copy(blk4[:, :, 0, :], be(ni[:, 0, :]))
                eng.tensor_copy(blk4[:, :, 1, :], be(nat_f[:, 0:ROW]))
                eng.tensor_copy(blk4[:, :, 2, :], be(ni[:, 2, :]))
                eng.tensor_copy(blk4[:, :, 3, :], be(nat_w[:, :]))
                eng.wait_ge(prep, next(step))
                eng.scalar_tensor_tensor(out=blk4[:, :, 4, :], in0=be(same[:, :]), scalar=-2 * NPAD, in1=be(nat_f[:, 0:ROW]),
                                         op0=ALU.mult, op1=ALU.add).then_inc(blk_ready, 1)
                for w in range(1, NT + 1):
                    if w > 4:
                        eng.wait_ge(cnt_ready, w - 4)
                    eng.tensor_scalar(junk[0:ER, w % 4 * ROW:(w % 4 + 1) * ROW], nat_f[:, 0:ROW], float(w * WIN), 0.0,
                                      ALU.is_lt, ALU.add, accum_out=cnt[:, w:w + 1]).then_inc(cnt_ready, 1)
                eng.wait_ge(starts_ready, 1)
                eng.wait_ge(cnt_ready, NT)
                eng.tensor_copy(s_f[:, :], bank(3)[0:NGR, 0:NT + 1]).then_inc(prep, 1)
                eng.wait_ge(prep, next(step))
                eng.tensor_copy(s_i[:, :], s_f[:, :]).then_inc(starts_read, 1)
                eng.wait_ge(starts_read, 1)
                eng.tensor_scalar(fb_i[:, :], s_i[:, :], BLK.bit_length() - 1, None, ALU.arith_shift_right).then_inc(prep, 1)
                eng.wait_ge(prep, next(step))
                eng.tensor_copy(fb[:, :], fb_i[:, :]).then_inc(prep, 1)
                eng.wait_ge(prep, next(step))
                eng.scalar_tensor_tensor(out=nsl[:, :], in0=fb[:, 0:NT], scalar=float(-BLK), in1=s_f[:, 1:NT + 1],
                                         op0=ALU.mult, op1=ALU.add).then_inc(prep, 1)
                eng.wait_ge(prep, next(step))
                eng.tensor_scalar(nsl_i[:, :], nsl[:, :], float(P - 1), None, ALU.add).then_inc(prep, 1)
                eng.wait_ge(prep, next(step))
                eng.tensor_scalar(nsl_i[:, :], nsl_i[:, :], P.bit_length() - 1, None, ALU.arith_shift_right).then_inc(prep, 1)
                eng.wait_ge(prep, next(step))
                eng.tensor_copy(nsl[:, :], nsl_i[:, :]).then_inc(prep, 1)
                eng.wait_ge(prep, next(step))
                eng.tensor_tensor_scan(cum[:, :], nsl[:, :], zero[:, :], 0.0, ALU.add, ALU.add).then_inc(prep, 1)
                eng.wait_ge(prep, next(step))
                for k in range(SG):
                    eng.tensor_scalar(junk[0:NGR, k * NT:(k + 1) * NT], cum[:, :], jf[:, k:k + 1], 0.0, ALU.is_le, ALU.add,
                                      accum_out=wf[:, k:k + 1])
                    ins = eng.scalar_tensor_tensor(out=junk[0:NGR, 256 + k * NT:256 + (k + 1) * NT], in0=cum[:, :],
                                                   scalar=jf[:, k:k + 1], in1=nsl[:, :], op0=ALU.is_le, op1=ALU.mult,
                                                   accum_out=cp[:, k:k + 1])
                ins.then_inc(prep, 1)
                eng.wait_ge(prep, next(step))
                for k in range(SG):
                    ins = eng.scalar_tensor_tensor(out=junk[0:NGR, 512 + k * (NT + 1):512 + (k + 1) * (NT + 1)], in0=iof[0:NGR, 0:NT + 1],
                                                   scalar=wf[:, k:k + 1], in1=fb[:, :], op0=ALU.is_equal, op1=ALU.mult,
                                                   accum_out=sb0[:, k:k + 1])
                ins.then_inc(prep, 1)
                eng.tensor_scalar(w0[:, :], wf[:, :], float(WIN), None, ALU.mult)
                eng.tensor_copy(w_i[:, :], wf[:, :])
                eng.tensor_tensor(cp[:, :], jf[:, :], cp[:, :], ALU.subtract).then_inc(prep, 1)
                eng.wait_ge(prep, next(step))
                eng.wait_ge(prep, next(step))
                eng.scalar_tensor_tensor(out=sb0[:, :], in0=cp[:, :], scalar=float(RB), in1=sb0[:, :],
                                         op0=ALU.mult, op1=ALU.add).then_inc(prep, 1)
                eng.wait_ge(prep, next(step))
                eng.tensor_tensor(wantf[:, :].rearrange("p (k r) -> p k r", k=SG), bi(sb0[:, :], RB),
                                  rf[:, :].rearrange("p (k r) -> p k r", k=SG), ALU.add).then_inc(prep, 1)
                eng.wait_ge(prep, next(step))
                eng.tensor_scalar(want_i[:, :], wantf[:, :], float(NB), None, ALU.min).then_inc(want_ready, 1)

                def stats(i):
                    for k in range(GN):
                        ins = eng.bn_stats(st3[:, k, :], x[:, bass.ds((i * GN + k) * D, D)])
                    ins.then_inc(bn, 1)
                    eng.wait_ge(bn, 2 * i + 1)
                    eng.sem_inc(hop_v, 1)
                    for k in range(GN):
                        ins = eng.bn_aggr(mv3[:, k, :], st3[:, k, :])
                    ins.then_inc(bn, 1)
                    eng.wait_ge(bn, 2 * i + 2)
                    eng.tensor_scalar(ve[:, :], mv3[:, :, 1], 1e-5, None, ALU.add).then_inc(var_ready, 1)
                    eng.wait_ge(sd_ready, i + 1)
                    eng.reciprocal(rs[:, :], sd[:, :]).then_inc(rs_ready, 1)
                    eng.wait_ge(rs_ready, i + 1)
                    eng.scalar_tensor_tensor(out=nb[:, :], in0=mv3[:, :, 0], scalar=-1.0, in1=rs[:, :],
                                             op0=ALU.mult, op1=ALU.mult).then_inc(nb_ready, 1)

                def turn(i):
                    eng.wait_ge(t_ready, i + 1)
                    src = bank(0, 2).rearrange("p (k c) -> p k c", k=GN)[:, :, 0:2 * WIN]
                    eng.sem_inc(hop_v, 1)
                    eng.tensor_copy(hT[:, :].rearrange("p (k c) -> p k c", k=GN), src).then_inc(hT_ready, 1)

                def take(i):
                    eng.wait_ge(mm_ready, i + 1)
                    eng.wait_ge(hpb_free, i + 1)
                    eng.tensor_tensor(hpb[:, :].rearrange("p (k d) -> p k d", k=GN),
                                      bank(2, 2)[0:WIN, :].rearrange("p (k d) -> p k d", k=GN),
                                      bc(bpool[:, :], GN), ALU.add).then_inc(evac, 1)
                    eng.wait_ge(xb_ready, i + 1)
                    xg = x[:, bass.ds(i * GN * D, GN * D)]
                    eng.tensor_tensor(xg, bank(4, 2)[0:WIN, :], xg, ALU.add).then_inc(evac, 1)

                eng.wait_ge(x_in, 32)
                eng.wait_ge(bias_in, 48)
                stats(0)
                with eng.Fori(0, NG - 1) as i:
                    turn(i)
                    stats(i + 1)
                    take(i)
                turn(NG - 1)
                take(NG - 1)

                eng.wait_ge(nat_in, 32)
                eng.tensor_copy(dsts[:, 0:1], prev[:, :])
                eng.tensor_copy(dsts[:, 1:GW + 1].rearrange("p (b e) -> p b e", e=BLK), nat4[:, :, 1, :])
                for f in (0, 2, 3):
                    ins = eng.tensor_copy(flds3[:, f, :].rearrange("p (b e) -> p b e", e=BLK), nat4[:, :, f, :])
                ins.then_inc(prep, 1)
                w0b = bi(w0[:, :], P)
                eng.wait_ge(prep, next(step))
                eng.tensor_tensor(flds3[:, 1, :].rearrange("p (k e) -> p k e", k=SG),
                                  dsts[:, 1:GW + 1].rearrange("p (k e) -> p k e", k=SG), w0b, ALU.subtract)
                eng.tensor_tensor(eqp[:, :], dsts[:, 1:GW + 1], dsts[:, 0:GW], ALU.is_equal)
                e4 = flds3[:, 4, :]
                eng.tensor_copy(e4.rearrange("p (b e) -> p b e", e=BLK), nat4[:, :, 4, :]).then_inc(prep, 1)
                eng.wait_ge(prep, next(step))
                e4k = e4.rearrange("p (k e) -> p k e", k=SG)
                eng.tensor_tensor(e4k, e4k, w0b, ALU.subtract).then_inc(flds_ready, 1)
                eng.tensor_copy(row_n[:, :], flds3[:, 1, :]).then_inc(rows_ready, 1)
                eng.tensor_copy(row_t[:, :], flds3[:, 2, :]).then_inc(rows_ready, 1)
                eng.tensor_scalar(row_s[:, :], eqp[:, :], -1.0, NEG, ALU.add, ALU.mult).then_inc(rows_ready, 1)
                eng.memset(acc[:, :], 0.0)
                for f in range(FLD):
                    eng.wait_ge(cols_ready, f + 1)
                    src = bank(f)[:, 0:SG * NGR].rearrange("p (k g) -> p g k", k=SG)
                    if f == 0:
                        eng.tensor_copy(srcs[:, :].rearrange("p (g k) -> p g k", k=SG), src)
                    else:
                        at = {3: 0, 4: 1, 2: 2, 1: 3}[f]
                        eng.tensor_copy(edgef4[:, :, at, :], src)

        def has(g):
            return not isinstance(g, int) or 0 <= g < NGR

        def wait(eng, sem, n):
            if not isinstance(n, int) or n > 0:
                eng.wait_ge(sem, n)

        def over_groups(eng, step, ring, lag, ahead=0, back=4):
            first = -(-back // ring) * ring
            turns = (NGR - ahead - first) // ring
            for g in range(first):
                step(g, g % ring, g // ring)
            with eng.Fori(0, turns) as i:
                for r in range(ring):
                    step(i * ring + (first + r), r, i + first // ring)
            for g in range(first + turns * ring, NGR + lag):
                step(g, g % ring, g // ring)

        load_no = count()

        def windows(eng, g):
            n = next(load_no)
            regs = [eng.alloc_register(name=f"win{n}_{k}") for k in range(SG)]
            eng.load(regs, wins[0:1, bass.ds(g * SG, SG)])
            return [eng.snap(r, donate=True, min_val=0, max_val=NT) for r in regs]

        b2 = ExitStack()
        with b2:
            def s2(name, shape, dt):
                return [sbt(f"{name}{r}", shape, dt, b2) for r in range(2)]

            def sem2(name):
                return b2.enter_context(nc.semaphore(name))

            gath = s2("gath", [P, SG * D], fp32)
            curi = s2("curi", [P, SG], i32)
            gw = s2("gw", [P, SG * D], fp32)
            mask = s2("mask", [P, GW], bf16)
            scan = s2("scan", [P, 2 * GW], fp32)
            rowm = s2("rowm", [P, SG * D], fp32)
            ends = s2("ends", [P, SG * WIN], fp32)
            cur_ready = sem2("cur_ready")
            got = [sem2(f"got{r}") for r in range(2)]
            mask_in = [sem2(f"mask_in{r}") for r in range(2)]
            gw_ready = sem2("gw_ready")
            turned = sem2("turned")
            scanned = sem2("scanned")
            unturned = sem2("unturned")
            rows_back = sem2("rows_back")
            ends_ready = sem2("ends_ready")
            selected = sem2("selected")
            summed = sem2("summed")
            hop_p2 = sem2("hop_p2")
            hop_a2 = sem2("hop_a2")
            block = b2.enter_context(nc.Block())

            @block.sync
            def _(eng):
                def step(g, r, n):
                    wait(eng, scanned, (g - 1) * 2)
                    eng.dma_start(mask[r][:, :], prow(start_row_d[bass.ds(g * GW, GW)], P)).then_inc(mask_in[r], 16)
                over_groups(eng, step, 2, 0, back=6)

            @block.gpsimd
            def _(eng):
                def step(g, r, n):
                    eng.wait_ge(cur_ready, g + 1)
                    wait(eng, gw_ready, g - 1)
                    eng.sem_inc(hop_p2, 1)
                    for k in range(SG):
                        eng.indirect_dma_start(gath[r][:, k * D:(k + 1) * D], None, hp_d[:, :],
                                               bass.IndirectOffsetOnAxis(ap=curi[r][:, k:k + 1], axis=0)).then_inc(got[r], 16)
                over_groups(eng, step, 2, 0, back=6)

            @block.scalar
            def _(eng):
                for r in range(2):
                    eng.activation(curi[r][:, :], srcs[:, r * SG:(r + 1) * SG], ACT.Copy).then_inc(cur_ready, 1)

                def step(g, r, n):
                    if has(g):
                        eng.wait_ge(got[r], (n + 1) * (16 * SG))
                        wait(eng, turned, g - 1)
                        eng.sem_inc(hop_a2, 1)
                        for k in range(SG):
                            ins = eng.activation(gw[r][:, k * D:(k + 1) * D], gath[r][:, k * D:(k + 1) * D], ACT.Copy,
                                                 scale=edgef[:, bass.ds(g * (4 * SG) + k, 1)])
                        ins.then_inc(gw_ready, 1)
                    if has(g + 2):
                        eng.activation(curi[r][:, :], srcs[:, bass.ds(g * SG + 2 * SG, SG)], ACT.Copy).then_inc(cur_ready, 1)
                    if has(g - 2):
                        wait(eng, selected, g - 3)
                        eng.wait_ge(unturned, g - 1)
                        eng.activation(rowm[r][:, :], bank(4, 2), ACT.Copy).then_inc(rows_back, 1)
                over_groups(eng, step, 2, 2, 2, back=6)

            @block.tensor
            def _(eng):
                def step(g, r, n):
                    if has(g):
                        wait(eng, scanned, (g - 1) * 2)
                        eng.wait_ge(gw_ready, g + 1)
                        for k in range(SG):
                            for hf in range(2):
                                ins = eng.transpose(bank(2 * r + hf)[:, k * P:(k + 1) * P],
                                                    gw[r][:, k * D + hf * P:k * D + hf * P + P], ident[:, :])
                        ins.then_inc(turned, 1)
                    if has(g - 1):
                        wait(eng, rows_back, g - 1)
                        eng.wait_ge(scanned, g * 2)
                        for k in range(SG):
                            for hf in range(2):
                                ins = eng.transpose(bank(4, 2)[:, k * D + hf * P:k * D + hf * P + P],
                                                    scan[1 - r][:, hf * GW + k * P:hf * GW + (k + 1) * P], ident[:, :])
                        ins.then_inc(unturned, 1)
                    if has(g - 3):
                        eng.wait_ge(ends_ready, g - 2)
                        eng.wait_ge(rows_back, g - 2)
                        for k in range(SG):
                            if k % 2 == 0:
                                wait(eng, summed, (g - 4) * SG + k + 2 if not isinstance(g, int) or g > 3 else 0)
                            for hf in range(2):
                                ins = eng.matmul(bank(6, 2)[:, k * 256 + hf * WIN:k * 256 + (hf + 1) * WIN],
                                                 rowm[1 - r][:, k * D + hf * P:k * D + hf * P + P],
                                                 ends[1 - r][:, k * WIN:(k + 1) * WIN], start=True, stop=True)
                        ins.then_inc(selected, 1)
                over_groups(eng, step, 2, 3, back=6)

            @block.vector
            def _(eng):
                def step(g, r, n):
                    if has(g - 4):
                        w = windows(eng, g - 4)
                        eng.wait_ge(selected, g - 3)
                    for k in range(SG):
                        if has(g - 4):
                            to = acc[:, bass.ds(w[k] * ACW0, ACW0)]
                            wait(eng, summed, (g - 4) * SG + k)
                            eng.tensor_tensor(to, bank(6, 2)[:, k * 256:k * 256 + ACW0], to, ALU.add).then_inc(summed, 1)
                        if has(g - 2):
                            ins = eng.tensor_scalar(ends[r][:, k * WIN:(k + 1) * WIN], iof[:, 0:WIN],
                                                    edgef[:, bass.ds((g - 2) * (4 * SG) + SG + k, 1)], None, ALU.is_equal)
                    if has(g - 2):
                        ins.then_inc(ends_ready, 1)
                    if has(g):
                        eng.wait_ge(mask_in[r], (n + 1) * 16)
                        wait(eng, unturned, g - 1)
                        wait(eng, scanned, g * 2)
                        eng.wait_ge(turned, g + 1)
                        for hf in range(2):
                            start = 0.0 if isinstance(g, int) and g == 0 else scan[1 - r][:, (hf + 1) * GW - 1:(hf + 1) * GW]
                            eng.tensor_tensor_scan(scan[r][:, hf * GW:(hf + 1) * GW], mask[r][:, :], bank(2 * r + hf),
                                                   start, ALU.add, ALU.max).then_inc(scanned, 1)
                over_groups(eng, step, 2, 4, back=6)

        def has_tiles(i):
            return not isinstance(i, int) or 0 <= i < NG

        def over_tiles(eng, step, lag=1, ahead=0):
            step(0)
            with eng.Fori(0, NG - 1 - ahead) as i:
                step(i + 1)
            for i in range(NG - ahead, NG + lag):
                step(i)

        qw = sbt("qw", [P, (NT + 1) * 3 * D], bf16)
        qw3 = qw[:, :].rearrange("p (w c) -> p w c", w=NT + 1)
        up = sbt("up", [WIN, NT * D], fp32)
        mc = sbt("mc", [P, 2 * D], fp32)
        em = sbt("em", [TY, D], fp32)
        c2 = sbt("c2", [WIN, D], fp32)
        upw2 = sbt("upw2", [P, 2 * D], fp32)
        w2b = sbt("w2b", [P, D], fp32)
        b2c = sbt("b2c", [P, 1], fp32)
        esc = sbt("esc", [P, 1], fp32)

        b3 = ExitStack()
        with b3:
            def s(name, shape, dt):
                return sbt(name, shape, dt, b3)

            def sem(name):
                return b3.enter_context(nc.semaphore(name))

            attw = s("attw", [P, 8 * D], fp32)
            upw1 = s("upw1", [P, 4 * D], fp32)
            msgw = s("msgw", [P, 2 * D], fp32)
            msgwT = s("msgwT", [P, 2 * D], fp32)
            vw = s("vw", [P, 2 * D], fp32)
            aw1 = s("aw1", [P, 2 * 2 * D], fp32)
            aw2 = s("aw2", [P, 4 * 2 * D], fp32)
            cols = s("cols", [P, 20], fp32)
            emb = s("emb", [TY, D], fp32)
            embT = s("embT", [P, 2 * TY], fp32)
            taskB = s("taskB", [P, 2 * TY], fp32)
            c1B = s("c1B", [P, 2 * TY], fp32)
            ubB = s("ubB", [P, 2 * WIN], fp32)
            ab1 = s("ab1", [TY, D], fp32)
            upb1 = s("upb1", [WIN, D], fp32)
            v1 = s("v1", [P, 4], fp32)
            v2 = s("v2", [P, 8], fp32)
            v3 = s("v3", [P, 4], fp32)
            gain = s("gain", [P, 4], fp32)
            c1 = s("c1", [P, 2], fp32)
            rsb = s("rsb", [TY, D], fp32)
            rres = s("rres", [TY, 2 * D], fp32)
            rpart = s("rpart", [TY, 3 * D], bf16)
            st = s("st_b", [WIN, GN * 6], fp32)
            mv = s("mv_b", [WIN, GN * 2], fp32)
            ve = s("ve_b", [WIN, GN], fp32)
            sd = s("sd_b", [WIN, GN], fp32)
            rs = s("rs_b", [WIN, GN], fp32)
            nb = s("nb_b", [WIN, GN], fp32)
            h = s("h_b", [WIN, GN * D], fp32)
            pb = s("pb", [WIN, GN * D], fp32)
            hT = s("hT_b", [P, GN * 2 * WIN], fp32)
            nT = s("nT", [P, GN * ACW0], fp32)
            qr = s("qr", [WIN, GN * D], fp32)
            st3 = st[:, :].rearrange("p (k c) -> p k c", k=GN)
            mv3 = mv[:, :].rearrange("p (k c) -> p k c", k=GN)
            params_in = sem("params_in")
            ua_free = sem("ua_free")
            ua_in = sem("ua_in")
            tps = sem("tps")
            tv = sem("tv")
            ta = sem("ta")
            r_in = sem("r_in")
            nt_ready = sem("nt_ready")
            n_ready = sem("n_ready")
            x1_ready = sem("x1_ready")
            bn = sem("bn_b")
            var_ready = sem("var_ready_b")
            sd_ready = sem("sd_ready_b")
            rs_ready = sem("rs_ready_b")
            nb_ready = sem("nb_ready_b")
            h_ready = sem("h_ready_b")
            t_ready = sem("t_ready_b")
            hT_ready = sem("hT_ready_b")
            pqu_ready = sem("pqu_ready")
            p_out = sem("p_out")
            q_hi = sem("q_hi")
            u_out = sem("u_out")
            q_res = sem("q_res")
            q_mid = sem("q_mid")
            q_res2 = sem("q_res2")
            q_low = sem("q_low")
            h_stored = sem("h_stored")
            p_stored = sem("p_stored")
            hop_s = sem("hop_s_b")
            hop_a = sem("hop_a_b")
            hop_v = sem("hop_v_b")
            hop_p = sem("hop_p_b")
            block = b3.enter_context(nc.Block())
            task, mab1, mab2, uab1, uab2, msgb = (cols[:, a:b] for a, b in ((0, 2), (2, 6), (6, 10), (10, 14), (14, 18), (18, 20)))
            NPAR = 20
            T_TASK, T_EMB, T_MA1, T_MA2, T_UA1, T_UA2, T_GAIN, T_VW, T_RPART, T_MC = range(1, 11)

            @block.sync
            def _(eng):
                def rows(t, name, k):
                    eng.dma_start(t.rearrange("p (k n) -> p k n", k=k),
                                  A[name].rearrange("(k p) n -> p k n", p=P)).then_inc(params_in, 16)
                rows(aw1[:, :], "L1_gnn_ma_W1", 2)
                rows(aw2[:, :], "L1_gnn_ma_W2", 4)
                with nc.allow_non_contiguous_dma(reason="vectors of a few hundred elements as columns"):
                    for t, name in ((task, "L1_gnn_task_embedding"), (mab1, "L1_gnn_ma_b1"), (mab2, "L1_gnn_ma_b2"),
                                    (uab1, "L1_gnn_ua_b1"), (uab2, "L1_gnn_ua_b2"), (msgb, "L1_gnn_msg_b")):
                        eng.dma_start(t, A[name].rearrange("(k p) -> p k", p=P)).then_inc(params_in, 16)
                rows(attw[:, :], "L1_gnn_att_W1", 8)
                rows(upw1[:, :], "L1_gnn_up_W1", 4)
                rows(msgw[:, :], "L1_gnn_msg_W", 2)
                rows(upw2[:, :], "L1_gnn_up_W2", 2)
                eng.dma_start(emb[:, :], A["L1_gnn_edge_emb"]).then_inc(params_in, 16)
                eng.dma_start(ab1[:, :], prow(A["L1_gnn_att_b1"], TY)).then_inc(params_in, 16)
                eng.dma_start(upb1[:, :], prow(A["L1_gnn_up_b1"], WIN)).then_inc(params_in, 16)
                eng.dma_start(w2b[:, :], prow(A["L1_gnn_att_W2"].rearrange("d o -> (d o)"), P)).then_inc(params_in, 16)
                eng.dma_start(b2c[:, :], prow(A["L1_gnn_att_b2"], P)).then_inc(params_in, 16)
                es = A["L1_gnn_edge_scale"]
                eng.dma_start(esc[:, :], prow(es, P)).then_inc(params_in, 16)
                eng.wait_ge(ua_free, 1)
                eng.dma_start(aw1[:, :].rearrange("p (k n) -> p k n", k=2),
                              A["L1_gnn_ua_W1"].rearrange("(k p) n -> p k n", p=P)).then_inc(ua_in, 16)
                eng.dma_start(aw2[:, :].rearrange("p (k n) -> p k n", k=4),
                              A["L1_gnn_ua_W2"].rearrange("(k p) n -> p k n", p=P)).then_inc(ua_in, 16)
                eng.wait_ge(tv, T_RPART)
                eng.dma_start(qw3[WIN:P, :, :], bc(rpart[:, :], NT + 1)).then_inc(r_in, 16)
                eng.wait_ge(r_in, 16)

                def step(i):
                    if has_tiles(i):
                        to = ph_d[bass.ds(i * (GN * WIN), GN * WIN), :].rearrange("(k p) d -> p k d", p=WIN)
                        eng.wait_ge(h_ready, i + 1)
                        eng.sem_inc(hop_s, 1)
                        eng.dma_start(to[:, :, D:2 * D], h[:, :].rearrange("p (k d) -> p k d", k=GN)).then_inc(h_stored, 16)
                        eng.wait_ge(p_out, i + 1)
                        eng.sem_inc(hop_s, 1)
                        eng.dma_start(to[:, :, 0:D], pb[:, :].rearrange("p (k d) -> p k d", k=GN)).then_inc(p_stored, 16)
                over_tiles(eng, step, 0)
                eng.wait_ge(h_stored, 16 * NG)
                eng.wait_ge(p_stored, 16 * NG)

            @block.tensor
            def _(eng):
                eng.wait_ge(params_in, 16 * (NPAR - 2))
                for k in range(2):
                    ins = eng.transpose(bank(0)[:, k * TY:(k + 1) * TY], emb[:, k * P:(k + 1) * P], ident[0:TY, 0:TY])
                for jh in range(2):
                    for ih in range(2):
                        ins = eng.transpose(bank(1)[:, jh * D + ih * P:jh * D + ih * P + P],
                                            msgw[:, ih * D + jh * P:ih * D + jh * P + P], ident[:, :])
                ins.then_inc(tps, 1)

                def affine1(b):
                    for f in range(4):
                        for k in range(2):
                            ins = eng.matmul(bank(b)[:, f:f + 1], aw1[:, k * 2 * D + f * P:k * 2 * D + f * P + P],
                                             task[:, k:k + 1], start=k == 0, stop=k == 1)
                    ins.then_inc(tps, 1)

                def affine2(b):
                    for f in range(4):
                        for k in range(4):
                            ins = eng.matmul(bank(b)[:, f:f + 1], aw2[:, k * 2 * D + f * P:k * 2 * D + f * P + P],
                                             v1[:, k:k + 1], start=k == 0, stop=k == 3)
                    ins.then_inc(tps, 1)
                affine1(2)
                eng.wait_ge(tv, T_EMB)
                for k in range(2):
                    eng.matmul(bank(3)[0:TY, 0:D], embT[:, k * TY:(k + 1) * TY], attw[:, (4 + k) * D:(5 + k) * D], start=k == 0, stop=False)
                for k in range(2):
                    ins = eng.matmul(bank(3)[0:TY, 0:D], taskB[:, k * TY:(k + 1) * TY], attw[:, (6 + k) * D:(7 + k) * D],
                                     start=False, stop=k == 1)
                ins.then_inc(tps, 1)
                eng.wait_ge(ta, 1)
                affine2(4)
                eng.wait_ge(ua_in, 32)
                affine1(5)
                eng.wait_ge(ta, 2)
                affine2(6)
                eng.wait_ge(tv, T_VW)
                for ih in range(2):
                    for jh in range(2):
                        ins = eng.matmul(bank(7)[:, ih * D:(ih + 1) * D], msgwT[:, jh * D + ih * P:jh * D + ih * P + P],
                                         vw[:, jh * D:(jh + 1) * D], start=jh == 0, stop=jh == 1)
                ins.then_inc(tps, 1)
                for jh in range(2):
                    ins = eng.matmul(bank(1)[0:WIN, 0:D], ubB[:, jh * WIN:(jh + 1) * WIN], upw1[:, (2 + jh) * D:(3 + jh) * D],
                                     start=jh == 0, stop=jh == 1)
                ins.then_inc(tps, 1)
                eng.wait_ge(tv, T_MC)
                for k in range(2):
                    eng.matmul(bank(2)[0:TY, 0:D], embT[:, k * TY:(k + 1) * TY], mc[:, k * D:(k + 1) * D], start=k == 0, stop=False)
                for jh in range(2):
                    ins = eng.matmul(bank(2)[0:TY, 0:D], c1B[:, jh * TY:(jh + 1) * TY], upw1[:, (2 + jh) * D:(3 + jh) * D],
                                     start=False, stop=jh == 1)
                ins.then_inc(tps, 1)
                eng.wait_ge(tv, T_MC + 1)

                def step(i):
                    if has_tiles(i - 1):
                        eng.wait_ge(h_ready, i)
                        for k in range(GN):
                            for hf in range(2):
                                ins = eng.transpose(bank(0, 2)[:, k * 256 + hf * WIN:k * 256 + (hf + 1) * WIN],
                                                    h[:, k * D + hf * P:k * D + hf * P + P], ident[0:WIN, 0:WIN])
                        ins.then_inc(t_ready, 1)
                        eng.wait_ge(hT_ready, i)
                    if has_tiles(i):
                        eng.wait_ge(nt_ready, i + 1)
                        for k in range(GN):
                            for hf in range(2):
                                ins = eng.matmul(bank(0, 2)[0:WIN, k * D:(k + 1) * D],
                                                 nT[:, k * ACW0 + hf * WIN:k * ACW0 + (hf + 1) * WIN],
                                                 wn[:, hf * D:(hf + 1) * D], start=hf == 0, stop=hf == 1)
                        ins.then_inc(n_ready, 1)
                    if has_tiles(i - 1):
                        wait(eng, u_out, i - 1)
                        wait(eng, q_res, i - 1)
                        for b, w in ((4, attw[:, 2 * D:4 * D]), (2, attw[:, 0:2 * D]), (6, upw1[:, 0:2 * D])):
                            for k in range(GN):
                                for hf in range(2):
                                    ins = eng.matmul(bank(b, 2)[0:WIN, k * D:(k + 1) * D],
                                                     hT[:, (k * 2 + hf) * WIN:(k * 2 + hf + 1) * WIN],
                                                     w[:, hf * D:(hf + 1) * D], start=hf == 0, stop=hf == 1)
                            ins.then_inc(pqu_ready, 1)
                over_tiles(eng, step)

            @block.scalar
            def _(eng):
                for n in range(2):
                    eng.wait_ge(tv, (T_MA1, T_UA1)[n])
                    eng.activation(v1[:, :], v3[:, :], ACT.Gelu).then_inc(ta, 1)
                eng.wait_ge(tv, T_UA2)
                eng.activation(gain[:, 0:2], v2[:, 0:2], ACT.Tanh)
                eng.activation(gain[:, 2:4], v2[:, 4:6], ACT.Tanh).then_inc(ta, 1)

                def step(i):
                    if has_tiles(i):
                        eng.wait_ge(var_ready, i + 1)
                        eng.activation(sd[:, :], ve[:, :], ACT.Sqrt).then_inc(sd_ready, 1)
                        wait(eng, h_stored, i * 16)
                        eng.wait_ge(nb_ready, i + 1)
                        eng.sem_inc(hop_a, 1)
                        for k in range(GN):
                            ins = eng.activation(h[:, k * D:(k + 1) * D], x[:, bass.ds((i * GN + k) * D, D)], ACT.Relu,
                                                 scale=rs[:, k:k + 1], bias=nb[:, k:k + 1])
                        ins.then_inc(h_ready, 1)
                    if has_tiles(i - 1):
                        win = bass.ds((i - 1) * GN, GN)
                        qr3 = qr[:, :].rearrange("p (k d) -> p k d", k=GN)
                        eng.wait_ge(pqu_ready, i * 3 - 2)
                        eng.sem_inc(hop_a, 1)
                        eng.activation(qw3[0:WIN, win, 0:D],
                                       bank(4, 2)[0:WIN, :].rearrange("p (k d) -> p k d", k=GN), ACT.Copy).then_inc(q_hi, 1)
                        eng.wait_ge(q_res, i)
                        eng.sem_inc(hop_a, 1)
                        eng.activation(qw3[0:WIN, win, D:2 * D], qr3, ACT.Copy).then_inc(q_mid, 1)
                        eng.wait_ge(pqu_ready, i * 3 - 1)
                        wait(eng, p_stored, (i - 1) * 16)
                        eng.activation(pb[:, :], bank(2, 2)[0:WIN, :], ACT.Copy).then_inc(p_out, 1)
                        eng.wait_ge(q_res2, i)
                        eng.sem_inc(hop_a, 1)
                        eng.activation(qw3[0:WIN, win, 2 * D:3 * D], qr3, ACT.Copy).then_inc(q_low, 1)
                        eng.wait_ge(pqu_ready, i * 3)
                        eng.sem_inc(hop_a, 1)
                        eng.activation(up[:, bass.ds((i - 1) * (GN * D), GN * D)], bank(6, 2)[0:WIN, :], ACT.Copy).then_inc(u_out, 1)
                over_tiles(eng, step)

            @block.gpsimd
            def _(eng):
                def step(i):
                    wait(eng, n_ready, i)
                    eng.sem_inc(hop_p, 1)
                    eng.tensor_copy(nT[:, :], acc[:, bass.ds(i * (GN * ACW0), GN * ACW0)]).then_inc(nt_ready, 1)
                over_tiles(eng, step, 0)

            @block.vector
            def _(eng):
                one = count(1)
                done = sem("done_b")
                eng.memset(qw[:, NT * 3 * D:(NT + 1) * 3 * D], 0.0)
                eng.wait_ge(params_in, 16 * (NPAR - 2))
                for k in range(2):
                    ins = eng.tensor_copy(taskB[:, k * TY:(k + 1) * TY], task[:, k:k + 1].to_broadcast([P, TY]))
                ins.then_inc(tv, 1)
                eng.wait_ge(tps, 1)
                eng.tensor_copy(msgwT[:, :], bank(1))
                eng.tensor_copy(embT[:, :], bank(0)[:, 0:2 * TY]).then_inc(tv, 1)
                eng.wait_ge(tps, 2)
                eng.tensor_tensor(v3[:, :], bank(2)[:, 0:4], mab1, ALU.add).then_inc(tv, 1)
                eng.wait_ge(tps, 4)
                eng.tensor_tensor(v2[:, 0:4], bank(4)[:, 0:4], mab2, ALU.add).then_inc(tv, 1)
                eng.wait_ge(tv, T_MA2)
                eng.sem_inc(ua_free, 1)
                eng.wait_ge(tps, 5)
                eng.wait_ge(ta, 1)
                eng.tensor_tensor(v3[:, :], bank(5)[:, 0:4], uab1, ALU.add).then_inc(tv, 1)
                eng.wait_ge(tps, 6)
                eng.tensor_tensor(v2[:, 4:8], bank(6)[:, 0:4], uab2, ALU.add).then_inc(tv, 1)
                eng.wait_ge(ta, 3)
                eng.tensor_scalar(gain[:, :], gain[:, :], 0.5, 1.0, ALU.mult, ALU.add).then_inc(tv, 1)
                eng.wait_ge(tv, T_GAIN)
                eng.tensor_tensor(v3[:, 0:2], gain[:, 0:2], gain[:, 2:4], ALU.mult)
                eng.tensor_tensor(c1[:, :], msgb, gain[:, 0:2], ALU.mult)
                for k in range(2):
                    ins = eng.tensor_copy(ubB[:, k * WIN:(k + 1) * WIN], v2[:, 6 + k:7 + k].to_broadcast([P, WIN]))
                ins.then_inc(done, 1)
                eng.wait_ge(done, next(one))
                for k in range(2):
                    eng.tensor_scalar(vw[:, k * D:(k + 1) * D], upw1[:, (2 + k) * D:(3 + k) * D], v3[:, k:k + 1], None, ALU.mult)
                eng.tensor_tensor(c1[:, :], c1[:, :], v2[:, 2:4], ALU.add).then_inc(done, 1)
                eng.wait_ge(done, next(one))
                eng.tensor_tensor(c1[:, :], c1[:, :], gain[:, 2:4], ALU.mult).then_inc(done, 1)
                eng.wait_ge(done, next(one))
                for k in range(2):
                    ins = eng.tensor_copy(c1B[:, k * TY:(k + 1) * TY], c1[:, k:k + 1].to_broadcast([P, TY]))
                ins.then_inc(tv, 1)
                eng.wait_ge(tps, 3)
                eng.tensor_tensor(rsb[:, :], bank(3)[0:TY, 0:D], ab1[:, :], ALU.add).then_inc(done, 1)
                eng.wait_ge(done, next(one))
                eng.tensor_copy(rpart[:, 0:D], rsb[:, :]).then_inc(done, 1)
                eng.wait_ge(done, next(one))
                eng.tensor_tensor(rres[:, 0:D], rsb[:, :], rpart[:, 0:D], ALU.subtract).then_inc(done, 1)
                eng.wait_ge(done, next(one))
                eng.tensor_copy(rpart[:, D:2 * D], rres[:, 0:D]).then_inc(done, 1)
                eng.wait_ge(done, next(one))
                eng.tensor_tensor(rres[:, D:2 * D], rres[:, 0:D], rpart[:, D:2 * D], ALU.subtract).then_inc(done, 1)
                eng.wait_ge(done, next(one))
                eng.tensor_copy(rpart[:, 2 * D:3 * D], rres[:, D:2 * D]).then_inc(tv, 1)
                eng.wait_ge(tps, 8)
                eng.tensor_tensor(c2[:, :], bank(1)[0:WIN, 0:D], upb1[:, :], ALU.add)
                eng.tensor_copy(mc[:, :], bank(7)).then_inc(tv, 1)
                eng.wait_ge(tps, 9)
                eng.tensor_copy(em[:, :], bank(2)[0:TY, 0:D]).then_inc(tv, 1)

                def step(i):
                    if has_tiles(i - 1):
                        eng.wait_ge(t_ready, i)
                        eng.sem_inc(hop_v, 1)
                        eng.tensor_copy(hT[:, :].rearrange("p (k c) -> p k c", k=GN),
                                        bank(0, 2).rearrange("p (k c) -> p k c", k=GN)[:, :, 0:2 * WIN]).then_inc(hT_ready, 1)
                    if has_tiles(i):
                        eng.wait_ge(n_ready, i + 1)
                        xg = x[:, bass.ds(i * (GN * D), GN * D)]
                        eng.tensor_tensor(xg, bank(0, 2)[0:WIN, :], xg, ALU.add).then_inc(x1_ready, 1)
                        eng.wait_ge(x1_ready, i + 1)
                        eng.sem_inc(hop_v, 1)
                        for k in range(GN):
                            ins = eng.bn_stats(st3[:, k, :], x[:, bass.ds((i * GN + k) * D, D)])
                        ins.then_inc(bn, 1)
                        eng.wait_ge(bn, 2 * i + 1)
                        eng.sem_inc(hop_v, 1)
                        for k in range(GN):
                            ins = eng.bn_aggr(mv3[:, k, :], st3[:, k, :])
                        ins.then_inc(bn, 1)
                        eng.wait_ge(bn, 2 * i + 2)
                        eng.tensor_scalar(ve[:, :], mv3[:, :, 1], 1e-5, None, ALU.add).then_inc(var_ready, 1)
                        eng.wait_ge(sd_ready, i + 1)
                        eng.reciprocal(rs[:, :], sd[:, :]).then_inc(rs_ready, 1)
                        eng.wait_ge(rs_ready, i + 1)
                        eng.scalar_tensor_tensor(out=nb[:, :], in0=mv3[:, :, 0], scalar=-1.0, in1=rs[:, :],
                                                 op0=ALU.mult, op1=ALU.mult).then_inc(nb_ready, 1)
                    if has_tiles(i - 1):
                        wait(eng, q_low, i - 1)
                        eng.wait_ge(q_hi, i)
                        win = bass.ds((i - 1) * GN, GN)
                        qr3 = qr[:, :].rearrange("p (k d) -> p k d", k=GN)
                        eng.tensor_tensor(qr3, bank(4, 2)[0:WIN, :].rearrange("p (k d) -> p k d", k=GN),
                                          qw3[0:WIN, win, 0:D], ALU.subtract).then_inc(q_res, 1)
                        eng.wait_ge(q_mid, i)
                        eng.tensor_tensor(qr3, qr3, qw3[0:WIN, win, D:2 * D], ALU.subtract).then_inc(q_res2, 1)
                over_tiles(eng, step)

        b4 = ExitStack()
        with b4:
            RING = 6

            def ring4(name, shape, dt, n=RING):
                return [sbt(f"{name}{r}", shape, dt, b4) for r in range(n)]

            def sem4(name):
                return b4.enter_context(nc.semaphore(name))

            gath = ring4("gath1_", [P, SG * 2 * D], fp32)
            curi = ring4("curi1_", [P, SG], i32)
            key = ring4("key", [P, GW], bf16, 2)
            hot = ring4("hot", [P, GW], bf16, 2)
            place = ring4("place", [P, SG * P], fp32, 3)
            types = ring4("types", [P, SG * TY], fp32, 3)
            logit = ring4("logit", [P, SG], fp32, 3)
            ew = ring4("ew", [P, SG], fp32, 3)
            onec = sbt("onec", [P, 1], fp32, b4)
            zeroed = sem4("zeroed")
            cur_ready = sem4("cur_ready1")
            got = [sem4(f"got1_{r}") for r in range(RING)]
            key_in = [sem4(f"key_in{r}") for r in range(2)]
            hot_ready = sem4("hot_ready")
            z_ready = sem4("z_ready")
            z_added = sem4("z_added")
            gelu_ready = sem4("gelu_ready")
            logit_ready = sem4("logit_ready")
            delta_ready = sem4("delta_ready")
            ew_ready = sem4("ew_ready")
            match_ready = sem4("match_ready")
            place_ready = sem4("place_ready")
            sums_ready = sem4("sums_ready")
            summed = sem4("summed1")
            hop_p = sem4("hop_p4")
            hop_a = sem4("hop_a4")
            block = b4.enter_context(nc.Block())

            @block.sync
            def _(eng):
                def step(g, r, n):
                    wait(eng, hot_ready, g - 1)
                    key_r = key[r % 2]
                    eng.dma_start(key_r[0:WIN, :], prow(node_row_d[bass.ds(g * GW, GW)], WIN)).then_inc(key_in[r % 2], 16)
                    eng.dma_start(key_r[WIN:P, :], prow(type_row_d[bass.ds(g * GW, GW)], TY)).then_inc(key_in[r % 2], 16)
                over_groups(eng, step, RING, 0, back=6)

            @block.gpsimd
            def _(eng):
                def step(g, r, n):
                    eng.wait_ge(cur_ready, g + 1)
                    wait(eng, sums_ready, g - 5)
                    eng.sem_inc(hop_p, 1)
                    for k in range(SG):
                        eng.indirect_dma_start(gath[r][:, k * 2 * D:(k + 1) * 2 * D], None, ph_d[:, :],
                                               bass.IndirectOffsetOnAxis(ap=curi[r][:, k:k + 1], axis=0)).then_inc(got[r], 16)
                over_groups(eng, step, RING, 0, back=6)

            def z_of(r):
                return gath[r][:, :].rearrange("p (k d) -> p k d", k=SG)[:, :, 0:D]

            @block.scalar
            def _(eng):
                for r in range(RING):
                    eng.activation(curi[r][:, :], srcs[:, r * SG:(r + 1) * SG], ACT.Copy).then_inc(cur_ready, 1)
                eng.wait_ge(zeroed, 1)

                def step(g, r, n):
                    if has(g):
                        eng.wait_ge(z_ready, g + 1)
                        eng.activation(z_of(r)[:, 0:2, :], bank(2 * (r % 2)).rearrange("p (k d) -> p k d", k=2), ACT.Gelu)\
                           .then_inc(gelu_ready, 1)
                        eng.wait_ge(z_added, g + 1)
                        eng.activation(z_of(r)[:, 2:4, :], z_of(r)[:, 2:4, :], ACT.Gelu).then_inc(gelu_ready, 1)
                        if has(g + RING):
                            eng.activation(curi[r][:, :], srcs[:, bass.ds(g * SG + RING * SG, SG)], ACT.Copy).then_inc(cur_ready, 1)
                    if has(g - 1):
                        q = (r - 1) % 3
                        eng.wait_ge(logit_ready, g)
                        eng.activation(logit[q][:, :], logit[q][:, :], ACT.Tanh, bias=b2c[:, :]).then_inc(delta_ready, 1)
                        eng.wait_ge(delta_ready, g)
                        eng.activation(ew[q][:, :], logit[q][:, :], ACT.Identity, scale=esc[:, :], bias=onec[:, :]).then_inc(ew_ready, 1)
                        eng.wait_ge(ew_ready, g)
                        eng.wait_ge(match_ready, g)
                        for k in range(SG):
                            at = place[q][:, k * P:k * P + WIN]
                            ins = eng.activation(at, at, ACT.Copy, scale=ew[q][:, k:k + 1])
                        ins.then_inc(place_ready, 1)
                over_groups(eng, step, RING, 1, RING, back=6)

            @block.tensor
            def _(eng):
                def step(g, r, n):
                    if has(g):
                        w = windows(eng, g)
                        wait(eng, gelu_ready, (g - 1) * 2)
                        eng.wait_ge(hot_ready, g + 1)
                        eng.wait_ge(got[r], (n + 1) * (16 * SG))
                        for k in range(SG):
                            to = bank(2 * (r % 2), 2)[:, k * D:(k + 1) * D]
                            for part in range(3):
                                ins = eng.matmul(to, hot[r % 2][:, k * P:(k + 1) * P],
                                           qw[:, bass.ds(w[k] * (3 * D) + part * D, D)], start=part == 0,
                                           stop=part == 2 and k >= 2)
                            if k < 2:
                                ins = eng.matmul(to, ident[:, :], gath[r][:, k * 2 * D:k * 2 * D + D], start=False, stop=True)
                        ins.then_inc(z_ready, 1)
                    if has(g - 2):
                        q = (r - 2) % RING
                        wait(eng, summed, (g - 3) * SG)
                        eng.wait_ge(place_ready, g - 1)
                        for k in range(SG):
                            at = bank(4 + 2 * (r % 2), 2)[:, k * 256:(k + 1) * 256]
                            to = place[q % 3][:, k * P:k * P + WIN]
                            for hf in range(2):
                                eng.matmul(at[:, hf * WIN:(hf + 1) * WIN],
                                           gath[q][:, k * 2 * D + D + hf * P:k * 2 * D + D + hf * P + P], to, start=True, stop=True)
                            ins = eng.matmul(at[:, 2 * WIN:2 * WIN + TY], place[q % 3][:, k * P:(k + 1) * P],
                                             types[q % 3][:, k * TY:(k + 1) * TY], start=True, stop=True)
                        ins.then_inc(sums_ready, 1)
                over_groups(eng, step, RING, 2, back=6)

            @block.vector
            def _(eng):
                eng.memset(onec[:, :], 1.0)
                for r in range(3):
                    eng.memset(place[r][:, :], 0.0)
                eng.memset(acc[:, :], 0.0).then_inc(zeroed, 1)
                eng.wait_ge(zeroed, 1)

                def match_keys(g, r):
                    eng.wait_ge(key_in[r], (g - r) * 16 + 32 if isinstance(g, int) else g * 16 + (32 - r * 16))
                    eng.tensor_scalar(hot[r][:, :], key[r][:, :], pcol[:, 0:1], None, ALU.is_equal).then_inc(hot_ready, 1)
                match_keys(0, 0)

                def step(g, r, n):
                    if has(g - 3):
                        w = windows(eng, g - 3)
                    if has(g):
                        eng.wait_ge(z_ready, g + 1)
                        eng.tensor_tensor(z_of(r)[:, 2:4, :], bank(2 * (r % 2) + 1).rearrange("p (k d) -> p k d", k=2),
                                          z_of(r)[:, 2:4, :], ALU.add).then_inc(z_added, 1)
                        wait(eng, sums_ready, g - 2)
                        e0 = g * (4 * SG) + 2 * SG
                        eng.tensor_tensor(types[r % 3][:, :].rearrange("p (k t) -> p k t", k=SG), bc(iof[:, 0:TY], SG),
                                          bi(edgef[:, bass.ds(e0, SG)], TY), ALU.is_equal)
                        eng.tensor_tensor(place[r % 3][:, :].rearrange("p (k t) -> p k t", k=SG)[:, :, 0:WIN], bc(iof[:, 0:WIN], SG),
                                          bi(edgef[:, bass.ds(e0 + SG, SG)], WIN), ALU.is_equal).then_inc(match_ready, 1)
                    if has(g + 1):
                        match_keys(g + 1, (r + 1) % 2)
                    if has(g - 3):
                        eng.wait_ge(sums_ready, g - 2)
                    for k in range(SG):
                        if has(g - 3):
                            to = acc[:, bass.ds(w[k] * ACW1, ACW1)]
                            wait(eng, summed, (g - 3) * SG + k)
                            eng.tensor_tensor(to, bank(4 + 2 * ((r + 1) % 2), 2)[:, k * 256:k * 256 + ACW1], to, ALU.add)\
                               .then_inc(summed, 1)
                        if has(g):
                            if k % 2 == 0:
                                eng.wait_ge(gelu_ready, g * 2 + k // 2 + 1)
                            zk = gath[r][:, k * 2 * D:k * 2 * D + D]
                            ins = eng.tensor_tensor_reduce(zk, zk, w2b[:, :], 1.0, 0.0, ALU.mult, ALU.add,
                                                           logit[r % 3][:, k:k + 1])
                    if has(g):
                        ins.then_inc(logit_ready, 1)
                over_groups(eng, step, RING, 3, 1, back=6)

        b5 = ExitStack()
        with b5:
            def s(name, shape, dt):
                return sbt(name, shape, dt, b5)

            def sem(name):
                return b5.enter_context(nc.semaphore(name))

            deg = s("deg", [WIN, NT], fp32)
            rd = s("rd", [WIN, NT], fp32)
            sums = s("sums", [P, GN * ACW1], fp32)
            tt = s("tt", [TY, GN * WIN], fp32)
            ge = s("ge", [WIN, GN * D], fp32)
            gT = s("gT", [P, GN * 2 * WIN], fp32)
            h1 = [s(f"h1_{r}", [WIN, GN * D], fp32) for r in range(2)]
            upb2 = s("upb2", [WIN, D], fp32)
            lng = s("lng", [WIN, D], fp32)
            lnb = s("lnb", [WIN, D], fp32)
            st = s("st_c", [WIN, GN * 6], fp32)
            mv = s("mv_c", [WIN, GN * 2], fp32)
            mva = s("mva", [WIN, NT * 2], fp32)
            sd = s("sd_c", [WIN, NT], fp32)
            rs = s("rs_c", [WIN, NT], fp32)
            nb = s("nb_c", [WIN, NT], fp32)
            yn = [s(f"yn{r}", [WIN, GN * D], fp32) for r in range(2)]
            mva3 = mva[:, :].rearrange("p (t c) -> p t c", c=2)
            consts_in = sem("consts_in")
            h1_in = sem("h1_in")
            sums_at = sem("sums_at")
            tt_ready = sem("tt_ready")
            tt_out = sem("tt_out")
            b_ready = sem("b_ready")
            rd_ready = sem("rd_ready")
            uc_ready = sem("uc_ready")
            u_ready = sem("u_ready")
            ge_ready = sem("ge_ready")
            g_ready = sem("g_ready")
            gT_ready = sem("gT_ready")
            y_ps = sem("y_ps")
            y_ready = sem("y_ready")
            bn = sem("bn_c")
            ln = sem("ln_c")
            sd_ready = sem("sd_ready_c")
            hb_ready = sem("hb_ready")
            yn_ready = sem("yn_ready")
            gained = sem("gained")
            xb_ready = sem("xb_ready_c")
            out_ready = sem("out_ready")
            stored = sem("stored")
            hop_a = sem("hop_a_c")
            hop_v = sem("hop_v_c")
            hop_p = sem("hop_p_c")
            hop_s = sem("hop_s_c")
            block = b5.enter_context(nc.Block())

            @block.sync
            def _(eng):
                for t, name in ((upb2, "L1_gnn_up_b2"), (lng, "L1_gnn_ln_g"), (lnb, "L1_gnn_ln_b")):
                    eng.dma_start(t[:, :], prow(A[name], WIN)).then_inc(consts_in, 16)

                def load(i):
                    wait(eng, y_ready, i)
                    eng.sem_inc(hop_s, 1)
                    eng.dma_start(h1[0][:, :].rearrange("p (k d) -> p k d", k=GN),
                                  ph_d[bass.ds(i * (GN * WIN), GN * WIN), D:2 * D].rearrange("(k p) d -> p k d", p=WIN))\
                       .then_inc(h1_in, 16)
                over_tiles(eng, load, 0)

                def store(i):
                    eng.wait_ge(out_ready, i + 1)
                    eng.sem_inc(hop_s, 1)
                    eng.dma_start(out[bass.ds(i * (GN * WIN), GN * WIN), :].rearrange("(k p) d -> p k d", p=WIN),
                                  x3[:, bass.ds(i * GN, GN), :]).then_inc(stored, 16)
                with eng.Fori(0, NG - 1) as i:
                    store(i)
                eng.wait_ge(out_ready, NG)
                full = (NT - 1) * WIN
                eng.dma_start(out[(NG - 1) * GN * WIN:full, :].rearrange("(k p) d -> p k d", p=WIN),
                              x3[:, (NG - 1) * GN:NT - 1, :]).then_inc(stored, 16)
                eng.dma_start(out[full:N, :], x3[0:LAST, NT - 1, :]).then_inc(stored, 16)
                eng.wait_ge(stored, 16 * (NG + 1))

            @block.gpsimd
            def _(eng):
                eng.wait_ge(consts_in, 48)

                def step(i):
                    ug = up[:, bass.ds(i * (GN * D), GN * D)].rearrange("p (k d) -> p k d", k=GN)
                    eng.tensor_tensor(ug, ug, bc(c2[:, :], GN), ALU.add).then_inc(uc_ready, 1)
                    eng.wait_ge(h1_in, i * 16 + 16)
                    hg = h1[0][:, :].rearrange("p (k d) -> p k d", k=GN)
                    eng.tensor_tensor(hg, hg, bc(upb2[:, :], GN), ALU.add).then_inc(hb_ready, 1)
                    xg = x3[:, bass.ds(i * GN, GN), :]
                    eng.tensor_tensor(xg, xg, bc(lnb[:, :], GN), ALU.add).then_inc(xb_ready, 1)
                over_tiles(eng, step, 0)

            @block.tensor
            def _(eng):
                def step(i):
                    if has_tiles(i - 1):
                        eng.wait_ge(ge_ready, i)
                        for k in range(GN):
                            for hf in range(2):
                                ins = eng.transpose(bank(4, 2)[:, k * 256 + hf * WIN:k * 256 + (hf + 1) * WIN],
                                                    ge[:, k * D + hf * P:k * D + hf * P + P], ident[0:WIN, 0:WIN])
                        ins.then_inc(g_ready, 1)
                    if has_tiles(i):
                        eng.wait_ge(sums_at, i + 1)
                        for k in range(GN):
                            ins = eng.transpose(bank(0)[0:TY, k * WIN:(k + 1) * WIN],
                                                sums[0:WIN, k * ACW1 + 2 * WIN:k * ACW1 + ACW1], ident[0:WIN, 0:WIN])
                        ins.then_inc(tt_ready, 1)
                        wait(eng, u_ready, i)
                        eng.wait_ge(tt_out, i + 1)
                        for k in range(GN):
                            at = bank(2, 2)[0:WIN, k * D:(k + 1) * D]
                            for hf in range(2):
                                eng.matmul(at, sums[:, k * ACW1 + hf * WIN:k * ACW1 + (hf + 1) * WIN], mc[:, hf * D:(hf + 1) * D],
                                           start=hf == 0, stop=False)
                            ins = eng.matmul(at, tt[:, k * WIN:(k + 1) * WIN], em[:, :], start=False, stop=True)
                        ins.then_inc(b_ready, 1)
                    if has_tiles(i - 1):
                        eng.wait_ge(gT_ready, i)
                        for k in range(GN):
                            for hf in range(2):
                                ins = eng.matmul(bank(6, 2)[0:WIN, k * D:(k + 1) * D], gT[:, (k * 2 + hf) * WIN:(k * 2 + hf + 1) * WIN],
                                                 upw2[:, hf * D:(hf + 1) * D], start=hf == 0, stop=hf == 1)
                        ins.then_inc(y_ps, 1)
                over_tiles(eng, step)

            @block.scalar
            def _(eng):
                def sums_of(i):
                    wait(eng, b_ready, i)
                    eng.sem_inc(hop_a, 1)
                    eng.activation(sums[:, :], acc[:, bass.ds(i * (GN * ACW1), GN * ACW1)], ACT.Copy).then_inc(sums_at, 1)

                def step(i):
                    if has_tiles(i + 1):
                        sums_of(i + 1)
                    wait(eng, g_ready, i)
                    eng.wait_ge(u_ready, i + 1)
                    eng.sem_inc(hop_a, 1)
                    eng.activation(ge[:, :], up[:, bass.ds(i * (GN * D), GN * D)], ACT.Gelu).then_inc(ge_ready, 1)
                sums_of(0)
                over_tiles(eng, step, 0, 1)
                eng.wait_ge(ln, 1)
                eng.activation(sd[:, :], mva3[:, :, 1], ACT.Sqrt).then_inc(sd_ready, 1)
                eng.wait_ge(ln, 3)

                def norm(i):
                    wait(eng, gained, i)
                    eng.sem_inc(hop_a, 1)
                    for k in range(GN):
                        t = i * GN + k
                        ins = eng.activation(yn[0][:, k * D:(k + 1) * D], up[:, bass.ds(t * D, D)], ACT.Identity,
                                             scale=rs[:, bass.ds(t, 1)], bias=nb[:, bass.ds(t, 1)])
                    ins.then_inc(yn_ready, 1)
                over_tiles(eng, norm, 0)

            @block.vector
            def _(eng):
                a4 = acc[0:WIN, 0:NT * ACW1].rearrange("p (w c) -> p w c", c=ACW1)[:, :, 2 * WIN:ACW1]
                eng.tensor_reduce(deg[:, :], a4, AX.X, ALU.add).then_inc(rd_ready, 1)
                eng.wait_ge(rd_ready, 1)
                eng.tensor_scalar(deg[:, :], deg[:, :], 1.0, None, ALU.max).then_inc(rd_ready, 1)
                eng.wait_ge(rd_ready, 2)
                eng.reciprocal(rd[:, :], deg[:, :]).then_inc(rd_ready, 1)
                eng.wait_ge(rd_ready, 3)
                st3 = st[:, :].rearrange("p (k c) -> p k c", k=GN)
                mv3 = mv[:, :].rearrange("p (k c) -> p k c", k=GN)

                def step(i):
                    if has_tiles(i - 1):
                        eng.wait_ge(g_ready, i)
                        eng.sem_inc(hop_v, 1)
                        eng.tensor_copy(gT[:, :].rearrange("p (k c) -> p k c", k=GN),
                                        bank(4, 2).rearrange("p (k c) -> p k c", k=GN)[:, :, 0:2 * WIN]).then_inc(gT_ready, 1)
                    if has_tiles(i):
                        eng.wait_ge(tt_ready, i + 1)
                        eng.sem_inc(hop_v, 1)
                        eng.tensor_copy(tt[:, :], bank(0)[0:TY, 0:GN * WIN]).then_inc(tt_out, 1)
                        eng.wait_ge(uc_ready, i + 1)
                        eng.wait_ge(b_ready, i + 1)
                        for k in range(GN):
                            t = i * GN + k
                            ut = up[:, bass.ds(t * D, D)]
                            ins = eng.scalar_tensor_tensor(out=ut, in0=bank(2, 2)[0:WIN, k * D:(k + 1) * D],
                                                           scalar=rd[:, bass.ds(t, 1)], in1=ut, op0=ALU.mult, op1=ALU.add)
                        ins.then_inc(u_ready, 1)
                    if has_tiles(i - 1):
                        eng.wait_ge(hb_ready, i)
                        eng.wait_ge(y_ps, i)
                        yg = up[:, bass.ds((i - 1) * (GN * D), GN * D)]
                        eng.tensor_tensor(yg, bank(6, 2)[0:WIN, :], h1[0][:, :], ALU.add).then_inc(y_ready, 1)
                        eng.wait_ge(y_ready, i)
                        eng.sem_inc(hop_v, 1)
                        for k in range(GN):
                            ins = eng.bn_stats(st3[:, k, :], up[:, bass.ds((i - 1) * (GN * D) + k * D, D)])
                        ins.then_inc(bn, 1)
                        eng.wait_ge(bn, i * 3 - 2)
                        eng.sem_inc(hop_v, 1)
                        for k in range(GN):
                            ins = eng.bn_aggr(mv3[:, k, :], st3[:, k, :])
                        ins.then_inc(bn, 1)
                        eng.wait_ge(bn, i * 3 - 1)
                        eng.sem_inc(hop_v, 1)
                        eng.tensor_copy(mva[:, bass.ds((i - 1) * (GN * 2), GN * 2)], mv[:, :]).then_inc(bn, 1)
                over_tiles(eng, step)
                eng.wait_ge(bn, NG * 3)
                eng.tensor_scalar(mva3[:, :, 1], mva3[:, :, 1], 1e-5, None, ALU.add).then_inc(ln, 1)
                eng.wait_ge(sd_ready, 1)
                eng.reciprocal(rs[:, :], sd[:, :]).then_inc(ln, 1)
                eng.wait_ge(ln, 2)
                eng.scalar_tensor_tensor(out=nb[:, :], in0=mva3[:, :, 0], scalar=-1.0, in1=rs[:, :],
                                         op0=ALU.mult, op1=ALU.mult).then_inc(ln, 1)

                def put(i):
                    eng.wait_ge(yn_ready, i + 1)
                    eng.wait_ge(consts_in, 48)
                    wait(eng, out_ready, i)
                    yg = yn[0][:, :].rearrange("p (k d) -> p k d", k=GN)
                    eng.tensor_tensor(yn[1][:, :].rearrange("p (k d) -> p k d", k=GN), yg, bc(lng[:, :], GN), ALU.mult).then_inc(gained, 1)
                    eng.wait_ge(xb_ready, i + 1)
                    eng.wait_ge(gained, i + 1)
                    xg = x[:, bass.ds(i * (GN * D), GN * D)]
                    eng.tensor_tensor(xg, yn[1][:, :], xg, ALU.add).then_inc(out_ready, 1)
                over_tiles(eng, put, 0)


_OUTS = [((3125, 256), 'float32')]


def kernel(**inputs):
    import numpy as _np
    import concourse.bacc as _bacc
    from concourse import mybir as _mybir
    from concourse.bass_utils import run_bass_kernel_spmd as _run

    nc = _bacc.Bacc("TRN2", target_bir_lowering=False, num_devices=1)
    arrays, args = {}, {}
    for name in inputs:
        a = _np.ascontiguousarray(inputs[name])
        arrays[f"in_{name}_dram"] = a
        args[name] = nc.dram_tensor(f"in_{name}_dram", a.shape, _mybir.dt.from_np(a.dtype), kind="ExternalInput").ap()
    outs = []
    for i, (shape, dtype) in enumerate(_OUTS):
        dt = _mybir.dt.from_np(_np.dtype(dtype))
        outs.append(nc.dram_tensor(f"out_{i}_dram", shape, dt, kind="ExternalOutput").ap())
    gnn_two_layers(nc, args, outs[0])
    r = _run(nc, [arrays], core_ids=[0])
    return r.results[0]["out_0_dram"]
```
